# Optimizing a Trainium2 kernel written in Bass

```python
import numpy as np
import jax
import jax.numpy as jnp

def _softmax(x, axis=-1):
    return jax.nn.softmax(x, axis=axis)

def _gelu(x):
    return jax.nn.gelu(x, approximate=True)

def _silu(x):
    return jax.nn.silu(x)

def _sigmoid(x):
    return jax.nn.sigmoid(x)

def _layernorm(x, axis=-1, eps=1e-05):
    m = jnp.mean(x, axis=axis, keepdims=True)
    v = jnp.var(x, axis=axis, keepdims=True)
    return (x - m) / jnp.sqrt(v + eps)

def _scatter_add(tgt, idx, src, axis=0):
    return tgt.at[idx].add(src)

def _segment_sum(src, seg, n):
    return jax.ops.segment_sum(src, seg, n)
kernel_name = 'mk_prb_d1_jaxref_r4_74f626'

def setup_inputs(seed: int=0):
    np.random.seed(seed)
    _w = jnp.asarray

    def _L0_attn_setup():
        import jax, jax.numpy as jnp
        import numpy as np
        D_MODEL = 256
        N_HEADS = 16
        ORDER = 6
        P2 = 2 * ORDER - 1
        EPS_CLAMP = 1e-06
        EPS_DEN = 1e-07

        def _beta_np():
            j = np.arange(ORDER, dtype=np.float32)
            alpha = (j + 1.0) ** (-1.5)
            tail = np.flip(np.cumsum(np.flip(alpha)))
            beta = np.concatenate([np.zeros(1, np.float32), tail[1:].astype(np.float32), np.zeros(ORDER - 1, np.float32)])
            return beta / beta.sum()

        def _cheb(x):
            T = [jnp.ones_like(x), x]
            for _ in range(2, P2):
                T.append(2.0 * x * T[-1] - T[-2])
            return jnp.stack(T, axis=3)
        key = jax.random.key(seed)
        k1, k2, k3 = jax.random.split(key, 3)
        B, S, D = (2, 256, D_MODEL)
        x = jax.random.normal(k1, (B, S, D), dtype=jnp.float32)
        W_in = jax.random.normal(k2, (3 * D, D), dtype=jnp.float32) * 0.02
        W_out = jax.random.normal(k3, (D, D), dtype=jnp.float32) * 0.02
        return {'x': x, 'W_in': W_in, 'W_out': W_out}
    _L0_attn_in = _L0_attn_setup()

    def _L0_ffn_setup():
        import jax, jax.numpy as jnp
        import numpy as np
        H = 256
        I = 512
        E = 8
        B, S = (2, 1024)
        EPS = 1e-05
        INIT = 0.02

        def _layernorm(x, w, b):
            mu = jnp.mean(x, axis=-1, keepdims=True)
            var = jnp.mean(jnp.square(x - mu), axis=-1, keepdims=True)
            return (x - mu) * jax.lax.rsqrt(var + EPS) * w + b
        key = jax.random.key(seed)
        ks = jax.random.split(key, 9)
        return {'hidden_states': jax.random.normal(ks[0], (B, S, H), jnp.float32), 'ln_w': jnp.ones((H,), jnp.float32), 'ln_b': jnp.zeros((H,), jnp.float32), 'router_w': jax.random.normal(ks[1], (H, E), jnp.float32) * INIT, 'gate_w': jax.random.normal(ks[2], (E, H, I), jnp.float32) * INIT, 'up_w': jax.random.normal(ks[3], (E, H, I), jnp.float32) * INIT, 'down_w': jax.random.normal(ks[4], (E, I, H), jnp.float32) * INIT, 'sh_gate': jax.random.normal(ks[5], (H, I), jnp.float32) * INIT, 'sh_up': jax.random.normal(ks[6], (H, I), jnp.float32) * INIT, 'sh_down': jax.random.normal(ks[7], (I, H), jnp.float32) * INIT}
    _L0_ffn_in = _L0_ffn_setup()
    _d = {'L0_attn_x': _L0_attn_in['x'], 'L0_attn_W_in': _L0_attn_in['W_in'], 'L0_attn_W_out': _L0_attn_in['W_out'], 'L0_ffn_ln_w': _L0_ffn_in['ln_w'], 'L0_ffn_ln_b': _L0_ffn_in['ln_b'], 'L0_ffn_router_w': _L0_ffn_in['router_w'], 'L0_ffn_gate_w': _L0_ffn_in['gate_w'], 'L0_ffn_up_w': _L0_ffn_in['up_w'], 'L0_ffn_down_w': _L0_ffn_in['down_w'], 'L0_ffn_sh_gate': _L0_ffn_in['sh_gate'], 'L0_ffn_sh_up': _L0_ffn_in['sh_up'], 'L0_ffn_sh_down': _L0_ffn_in['sh_down']}
    _x0 = _d['L0_attn_x']
    _d['L0_attn_x'] = jax.random.normal(jax.random.fold_in(jax.random.key(seed), 1), (2, 2048, 256), dtype=_x0.dtype)
    del _x0
    return _d

def reference(L0_attn_x, L0_attn_W_in, L0_attn_W_out, L0_ffn_ln_w, L0_ffn_ln_b, L0_ffn_router_w, L0_ffn_gate_w, L0_ffn_up_w, L0_ffn_down_w, L0_ffn_sh_gate, L0_ffn_sh_up, L0_ffn_sh_down):

    def _L0_attn_ref(x, W_in, W_out):
        import jax, jax.numpy as jnp
        import numpy as np
        D_MODEL = 256
        N_HEADS = 16
        ORDER = 6
        P2 = 2 * ORDER - 1
        EPS_CLAMP = 1e-06
        EPS_DEN = 1e-07

        def _beta_np():
            j = np.arange(ORDER, dtype=np.float32)
            alpha = (j + 1.0) ** (-1.5)
            tail = np.flip(np.cumsum(np.flip(alpha)))
            beta = np.concatenate([np.zeros(1, np.float32), tail[1:].astype(np.float32), np.zeros(ORDER - 1, np.float32)])
            return beta / beta.sum()

        def _cheb(x):
            T = [jnp.ones_like(x), x]
            for _ in range(2, P2):
                T.append(2.0 * x * T[-1] - T[-2])
            return jnp.stack(T, axis=3)
        B, S, D = x.shape
        H, Dh = (N_HEADS, D // N_HEADS)
        qkv = jnp.einsum('bsd,ed->bse', x, W_in)
        q, k, v = jnp.split(qkv, 3, axis=-1)
        q = q.reshape(B, S, H, Dh).transpose(0, 2, 1, 3)
        k = k.reshape(B, S, H, Dh).transpose(0, 2, 1, 3)
        v = v.reshape(B, S, H, Dh).transpose(0, 2, 1, 3)
        inv_sqrt_d = 1.0 / jnp.sqrt(jnp.float32(Dh))
        xq = jnp.clip(q * inv_sqrt_d, -1.0 + EPS_CLAMP, 1.0 - EPS_CLAMP)
        xk = jnp.clip(k * inv_sqrt_d, -1.0 + EPS_CLAMP, 1.0 - EPS_CLAMP)
        Tq = _cheb(xq)
        Tk = _cheb(xk)
        beta = jnp.asarray(_beta_np())
        Tv = Tk * v[:, :, :, None, :]
        kv_prefix = jnp.cumsum(Tv, axis=2)
        ks_prefix = jnp.cumsum(Tk.sum(axis=-1), axis=2)
        kv_beta = kv_prefix * beta[None, None, None, :, None]
        k_beta = ks_prefix * beta[None, None, None, :]
        num = (Tq * kv_beta).sum(axis=3)
        den = (Tq.sum(axis=-1) * k_beta).sum(axis=3)
        out_h = num / (den[..., None] + EPS_DEN)
        out = out_h.transpose(0, 2, 1, 3).reshape(B, S, H * Dh)
        return jnp.einsum('bsd,ed->bse', out, W_out)

    def _L0_ffn_ref(hidden_states, ln_w, ln_b, router_w, gate_w, up_w, down_w, sh_gate, sh_up, sh_down):
        import jax, jax.numpy as jnp
        import numpy as np
        H = 256
        I = 512
        E = 8
        B, S = (2, 1024)
        EPS = 1e-05
        INIT = 0.02

        def _layernorm(x, w, b):
            mu = jnp.mean(x, axis=-1, keepdims=True)
            var = jnp.mean(jnp.square(x - mu), axis=-1, keepdims=True)
            return (x - mu) * jax.lax.rsqrt(var + EPS) * w + b
        b, s, h = hidden_states.shape
        normed = _layernorm(hidden_states, ln_w, ln_b)
        xf = normed.reshape(-1, h)
        logits = xf @ router_w
        top_idx = jnp.argmax(logits, axis=-1)
        top_score = jax.nn.sigmoid(jnp.max(logits, axis=-1))

        def body(acc, ew):
            g, u, d, e = ew
            w = jnp.where(top_idx == e, top_score, 0.0)[:, None]
            xe = xf * w
            hmid = jax.nn.silu(xe @ g) * (xe @ u)
            return (acc + hmid @ d, None)
        routed, _ = jax.lax.scan(body, jnp.zeros_like(xf), (gate_w, up_w, down_w, jnp.arange(E)))
        shared = jax.nn.silu(xf @ sh_gate) * (xf @ sh_up) @ sh_down
        moe_out = (routed + shared).reshape(b, s, h)
        return hidden_states + moe_out
    x = L0_attn_x
    xn = _layernorm(x, axis=-1)
    x = x + _L0_attn_ref(xn, L0_attn_W_in, L0_attn_W_out) + _L0_ffn_ref(xn, L0_ffn_ln_w, L0_ffn_ln_b, L0_ffn_router_w, L0_ffn_gate_w, L0_ffn_up_w, L0_ffn_down_w, L0_ffn_sh_gate, L0_ffn_sh_up, L0_ffn_sh_down)
    return x

_drawn_inputs = setup_inputs


def setup_inputs(seed=0):
    import zlib

    import numpy as np

    out = dict(_drawn_inputs(seed))
    spreads = {'L0_ffn_ln_w': (1.0, 0.6), 'L0_ffn_ln_b': (0.0, 0.8)}
    factors = {'L0_attn_W_in': 8.0,
     'L0_attn_W_out': 8.0,
     'L0_ffn_router_w': 8.0,
     'L0_ffn_gate_w': 8.0,
     'L0_ffn_up_w': 8.0,
     'L0_ffn_down_w': 8.0,
     'L0_ffn_sh_gate': 4.609,
     'L0_ffn_sh_up': 4.52,
     'L0_ffn_sh_down': 4.546}
    for name, (base, spread) in spreads.items():
        noise = np.random.default_rng([zlib.crc32(name.encode()), seed]).standard_normal(out[name].shape)
        drawn = base * np.exp(spread * noise) if base else spread * noise
        out[name] = jnp.asarray(drawn.astype(out[name].dtype))
    for name, factor in factors.items():
        out[name] = (out[name] * factor).astype(out[name].dtype)
    return out
```

```python
from contextlib import ExitStack

import numpy as np

import concourse.bass as bass
from concourse import mybir

ALU = mybir.AluOpType
ACT = mybir.ActivationFunctionType
AX = mybir.AxisListType.X
F32 = mybir.dt.float32
F32R = mybir.dt.float32r
I32 = mybir.dt.int32

P = 128
B, S, D = 2, 2048, 256
N = B * S
NT = N // P
BLK = 512
TPB = BLK // P
NB = N // BLK
UNIT = BLK // 2
TPU = UNIT // P
NC = D // P
HEADS = 16
DH = D // HEADS
I = 512
NI = I // P
E = 8
LN_EPS = 1e-5
M = 5
R = M * HEADS
HG = DH // NC
ST = NT + E - 1
PAIRS = (ST - 3) // 2
SLOTS = 2
WCOLS = 2 * NC * I + NI * D


def chebyshev_weights():
    order = 6
    j = np.arange(order, dtype=np.float32)
    alpha = (j + 1.0) ** (-1.5)
    tail = np.flip(np.cumsum(np.flip(alpha)))
    beta = np.concatenate([np.zeros(1, np.float32), tail[1:].astype(np.float32), np.zeros(order - 1, np.float32)])
    return [float(x) for x in (beta / beta.sum())[1:M + 1]]


BETA = chebyshev_weights()
SCALE = 16.0 / BETA[0]
A2, A3 = 4 * BETA[1] * SCALE, BETA[2] * SCALE
A4, A5 = 64 * BETA[3] * SCALE, 16 * BETA[4] * SCALE
DEN_EPS = 1e-7 * SCALE
CLIP = float(np.float32(1.0 - 1e-6)) * 4.0


def layout(*parts):
    at, where = 0, {}
    for name, width in parts:
        where[name] = (at, at + width)
        at += width
    return where, at


CONST, SENT_COLS = layout(
    ("ident", P), ("before", P), ("upto", P), ("ksum", M * R), ("qsum", M * R), ("tileno", E * ST))
SET, CONST_COLS = layout(
    ("sent", SENT_COLS), ("ones", P), ("kbias", TPU * R), ("qbias", TPU * R), ("restart", NC * (UNIT + 1)),
    ("mhalf", 1), ("mfive8", 1), ("s4bias", 1), ("r5bias", 1), ("keep", NB + 1), ("tilemask", E * NT), ("rank", E * NT))
CONST.update(SET)


def constants():
    c = np.zeros((P, SENT_COLS), np.float32)

    def put(name, value):
        a, b = CONST[name]
        c[:, a:b] = value.reshape(P, -1)

    put("ident", np.eye(P, dtype=np.float32))
    put("before", np.triu(np.ones((P, P), np.float32), 1))
    put("upto", np.triu(np.ones((P, P), np.float32)))
    feat = np.zeros((2, M, M))
    feat[0, 0, [0, 2, 4]] = 0.25, -0.75, -4 * 5 / 64
    feat[0, 1, 1] = 2.0
    feat[0, 2, 3] = 8.0
    feat[0, 3, 2] = 1.0
    feat[0, 4, 4] = 4.0
    feat[1] = feat[0] * np.array(BETA)[None, :] * SCALE
    feat[1, 1, 1] /= A3
    feat[1, 3, 2] /= A3
    feat[1, 2, 3] /= A4
    feat[1, 4, 4] /= A5
    for side, name in enumerate(("ksum", "qsum")):
        w = np.zeros((P, M, M, HEADS), np.float32)
        for ch in range(P):
            w[ch, :, :, ch // HG] = feat[side]
        put(name, w)
    put("tileno", np.broadcast_to(np.arange(ST, dtype=np.float32)[None, None], (P, E, ST)))
    return c


def token_layer_kernel(nc, consts, x, W_in, W_out, ln_w, ln_b, router_w, gate_w, up_w, down_w,
                       sh_gate, sh_up, sh_down, out):
    with ExitStack() as ctx:
        def sb(name, shape, dt=F32):
            return ctx.enter_context(nc.sbuf_tensor(name, shape, dt))

        def bank(name):
            return ctx.enter_context(nc.psum_tensor(name, [P, BLK], F32))

        def sem(name):
            return ctx.enter_context(nc.semaphore(name))

        x_rows = x.rearrange("b s d -> (b s) d")
        out_rows = out.rearrange("b s d -> (b s) d")
        expert_rows = nc.dram_tensor("expert_rows", [N + 1, D], F32, kind="Internal").ap()
        rest_rows = nc.dram_tensor("rest_rows", [N + 1, D], F32, kind="Internal").ap()
        table = nc.dram_tensor("table", [ST * P, 2], I32, kind="Internal").ap()

        def tiles_of(dram):
            return dram[0:N, :].rearrange("(t p) d -> p t d", p=P)

        cst = sb("cst", [P, CONST_COLS])

        def const(name, part=P):
            a, b = CONST[name]
            return cst[0:part, a:b]

        ident = const("ident")
        router = sb("router", [P, NC, E])
        ln_scale = sb("ln_scale", [P, NC])
        ln_shift = sb("ln_shift", [P, NC])
        gu_hi = sb("gu_hi", [P, 2 * NC * I], F32R)
        gu_lo = sb("gu_lo", [P, 2 * NC * I], F32R)
        down_s = sb("down_s", [P, NI, D])
        win_hi = sb("win_hi", [P, NC, 3, D], F32R)
        win_lo = sb("win_lo", [P, NC, 3, D], F32R)
        wout = sb("wout", [P, NC, D])
        experts = sb("experts", [P, SLOTS * WCOLS])
        work = sb("work", [P, 16, BLK])
        terms = sb("terms", [P, M, NC, UNIT + 1])
        run = sb("run", [P, M, NC, UNIT + 1])
        num = sb("num", [P, TPB // TPU, NC, UNIT])
        fsum = sb("fsum", [P, 2 * M, UNIT])
        x_now, x_next, xn, z, base, rest = [sb(n, [P, TPB, D]) for n in ("x_now", "x_next", "xn", "z", "base", "rest")]
        xT_raw = sb("xT_raw", [P, NC, BLK])
        xnT_hi, xnT_lo, xfT_hi, xfT_lo = [sb(n, [P, NC, BLK], F32R) for n in ("xnT_hi", "xnT_lo", "xfT_hi", "xfT_lo")]
        hid = sb("hid", [P, NI, BLK])
        silu = sb("silu", [P, BLK])
        ksb, qsb, acc, prod = [sb(n, [P, TPU * R]) for n in ("ksb", "qsb", "acc", "prod")]
        den = sb("den", [P, TPU * HEADS])
        recip = sb("recip", [P, TPU * HEADS])
        recip_wide = sb("recip_wide", [P, TPU * HEADS, HG])
        NS = 5
        stats = sb("stats", [P, (NB + 1) * TPB * NS])
        stats_now = sb("stats_now", [P, 2 * TPB * NS])
        logit = sb("logit", [P, E, NT])
        expert_ends = sb("expert_ends", [P, E])
        place = sb("place", [P, NT], I32)
        place_now = sb("place_now", [P, TPB], I32)
        entry = sb("entry", [P, NT * 2], I32)
        entry_now = sb("entry_now", [P, TPB * 2], I32)
        sorted_entry = sb("sorted_entry", [P, ST * 2], I32)
        seat_x, seat_r, seat_o = [sb(n, [P, 2], I32) for n in ("seat_x", "seat_r", "seat_o")]
        tile_needs = sb("tile_needs", [1, ST], I32)
        tile_at = sb("tile_at", [1, ST], I32)
        tiles_upto = sb("tiles_upto", [1, E], I32)

        def flat(ap):
            return ap.rearrange("p a b -> p (a b)")

        def pair(ap):
            return ap.rearrange("p (c n) -> p c n", c=NC)

        W = {name: work[:, n, :] for n, name in enumerate(
            ("kraw", "qraw", "uk", "yk", "sk", "rk", "uq", "yq3", "yq2", "sq", "rq", "uy", "ur", "t1", "t2", "t3"))}
        FS = {name: fsum[:, n, :] for n, name in enumerate(
            ("uk", "yk", "sk", "uyk", "urk", "uq", "yq3", "sq", "uyq", "urq"))}

        x_all = flat(work[:, :, :]).rearrange("p (t d) -> p t d", d=D)
        flat_run, flat_fsum = run[:, :, :, :].rearrange("p m c n -> p (m c n)"), flat(fsum[:, :, :])
        ring = [t[:, h * TPB * D:(h + 1) * TPB * D].rearrange("p (t d) -> p t d", d=D) for t in (flat_run, flat_fsum) for h in range(2)]
        logT = hid[0:E, 2, :]
        ring_T = (base, rest)
        raw_gate = experts[:, 0:NC * I]
        raw_up = experts[:, NC * I:2 * NC * I]
        raw_in = experts[:, 2048:2048 + 6 * D].rearrange("p (s c d) -> p s c d", s=3, c=NC)
        raw_out = experts[:, 3584:3584 + 2 * D].rearrange("p (r d) -> p r d", r=2)
        raw_out_c = experts[:, 4096:4096 + 2 * D].rearrange("p (r d) -> p r d", r=2)
        grids = experts[:, 4608:4608 + 6 * E * NT].rearrange("p (k n) -> p k n", k=6)
        moments6 = silu[:, 0:NT * 6].rearrange("p (t s) -> p t s", s=6)
        moments = silu[:, NT * 6:NT * 8].rearrange("p (t s) -> p t s", s=2)
        small = hid[:, 0, 0:10 * NT].rearrange("p (k t) -> p k t", t=NT)
        zero_row = prod[0:1, :]
        stat = stats[:, :].rearrange("p (t s) -> p t s", s=NS)
        best = hid[:, 1, 0:NT]

        e_rows = [work[:, k, 0:D] for k in range(2)]
        e_rest = [work[:, 2 + k, 0:D] for k in range(2)]
        e_xT = [work[:, 4 + k, 0:D] for k in range(2)]
        e_silu = work[:, 6, :]
        e_hid = [work[:, 7 + k, :] for k in range(2)]
        e_hT = work[:, 9, :]
        e_y = [work[:, 10 + k, 0:D] for k in range(2)]

        pK, pV, pQ, pG, pU, pS, pR, pT = [bank(n) for n in ("pK", "pV", "pQ", "pG", "pU", "pS", "pR", "pT")]
        ksum_at, qsum_at = pS[:, 0:TPU * R], pS[:, TPU * R:2 * TPU * R]
        prefix_at, spread_at = pR[:, 0:TPU * R], pR[:, UNIT:2 * UNIT]
        e_gate, e_up = (pK, pG), (pV, pU)

        x_loaded = [sem(f"x_loaded{b}") for b in range(NB)]
        first_loaded, const_loaded, in_loaded, raw_loaded, const_set, zero_set, pads_stored, passed = [
            sem(n) for n in ("first_loaded", "const_loaded", "in_loaded", "raw_loaded", "const_set", "zero_set", "pads_stored",
                             "passed")]
        stat_step, var_ready, root_ready, stats_ready = [sem(n) for n in ("stat_step", "var_ready", "root_ready", "stats_ready")]
        normed_ready, turned, zT_ready, logT_ps, logT_ready, logit_ps, logit_ready = [
            sem(n) for n in ("normed_ready", "turned", "zT_ready", "logT_ps", "logT_ready", "logit_ps", "logit_ready")]
        normed_stored = [sem(f"normed_stored{r}") for r in range(4)]
        gu_hi_ready, gu_lo_ready, out_sorted = sem("gu_hi_ready"), sem("gu_lo_ready"), sem("out_sorted")
        turned_w, whi_ready, wlo_ready, wout_ready = [sem(n) for n in ("turned_w", "whi_ready", "wlo_ready", "wout_ready")]
        route_step, onehot_ready, before_ps, best_ready, score_ready, place_ready, map_ready = [
            sem(n) for n in ("route_step", "onehot_ready", "before_ps", "best_ready", "score_ready", "place_ready", "map_ready")]
        x_now_in, x_next_in, now_copied, xn_ready, z_ready, base_ready = [
            sem(n) for n in ("x_now_in", "x_next_in", "now_copied", "xn_ready", "z_ready", "base_ready")]
        entry_copied, entries_stored = sem("entry_copied"), sem("entries_stored")
        pT_ps, pT_used, xnT_lo_ready, xfT_lo_ready = [sem(n) for n in ("pT_ps", "pT_used", "xnT_lo_ready", "xfT_lo_ready")]
        k_ps, v_ps, q_ps, v_used, kraw_ready, qraw_ready = [
            sem(n) for n in ("k_ps", "v_ps", "q_ps", "v_used", "kraw_ready", "qraw_ready")]
        uk_ready, yk_ready, sk_ready, rk_ready = [sem(n) for n in ("uk_ready", "yk_ready", "sk_ready", "rk_ready")]
        uq_ready, yq3_ready, yq2_ready, sq_ready, rq_ready = [
            sem(n) for n in ("uq_ready", "yq3_ready", "yq2_ready", "sq_ready", "rq_ready")]
        pool_step, kfeat_ready, qfeat_ready, ksum_ps, qsum_ps = [
            sem(n) for n in ("pool_step", "kfeat_ready", "qfeat_ready", "ksum_ps", "qsum_ps")]
        den_step, ksb_ready, qsb_ready, acc_kept, prefix_ps, recip_ready, wide_ready, spread_ps, quot_ready = [
            sem(n) for n in ("den_step", "ksb_ready", "qsb_ready", "acc_kept", "prefix_ps", "recip_ready", "wide_ready",
                             "spread_ps", "quot_ready")]
        g_ps, u_ps, silu_ready, hid_ready = [sem(n) for n in ("g_ps", "u_ps", "silu_ready", "hid_ready")]
        out_ps, rest_done, rest_stored, dve_step = sem("out_ps"), sem("rest_done"), sem("rest_stored"), sem("dve_step")
        w_landed = [sem(f"w_landed{e}") for e in range(E)]
        w_loaded, entries_back, seat_x_set, seat_r_set, seat_o_set = [
            sem(n) for n in ("w_loaded", "entries_back", "seat_x_set", "seat_r_set", "seat_o_set")]
        row_in = [sem(f"row_in{h}") for h in range(2)]
        rest_in = [sem(f"rest_in{h}") for h in range(2)]
        out_stored = [sem(f"out_stored{h}") for h in range(2)]
        eg_ps = sem("eg_ps")
        eu_ps = [sem(f"eu_ps{h}") for h in range(2)]
        xT_ps, xT_ready, esilu_ready, ehid_ready, hT_ps, hT_ready, y_ps, y_ready = [
            sem(n) for n in ("xT_ps", "xT_ready", "esilu_ready", "ehid_ready", "hT_ps", "hT_ready", "y_ps", "y_ready")]

        FIRSTS = 16 * (2 + 2 * NC)
        CONSTS = 16 * 2
        INS = 16 * (3 * NC + 1)
        RAWS = 16 * 3
        GROUPS, GB = 2, 4

        def steady(eng):
            eng.sem_inc(passed, 1)

        block = ctx.enter_context(nc.Block())

        @block.sync
        def _(sp):
            for b in range(NB):
                sp.dma_start(x_all[:, TPB * b:TPB * (b + 1), :],
                             tiles_of(x_rows)[:, TPB * b:TPB * (b + 1), :]).then_inc(x_loaded[b], 16)
                if b == 0:
                    sp.dma_start(ident, consts[:, 0:P]).then_inc(first_loaded, 16)
                    sp.dma_start(router[:, :, :], router_w.rearrange("(c p) e -> p c e", p=P)).then_inc(first_loaded, 16)
                    for c in range(NC):
                        sp.dma_start(ln_scale[:, c:c + 1], ln_w[c * P:(c + 1) * P].unsqueeze(1)).then_inc(first_loaded, 16)
                        sp.dma_start(ln_shift[:, c:c + 1], ln_b[c * P:(c + 1) * P].unsqueeze(1)).then_inc(first_loaded, 16)
            w_rows = W_in.rearrange("(s h c g) d -> s c h g d", s=3, c=NC, g=HG)
            for s in range(3):
                for c in range(NC):
                    sp.dma_start(raw_in[:, s, c, :], w_rows[s, c]).then_inc(in_loaded, 16)
            sp.dma_start(raw_out, W_out.rearrange("(r p) d -> p r d", p=P)).then_inc(in_loaded, 16)

            def load_block(into, b, done):
                sp.dma_start(into[:, :, :], tiles_of(x_rows)[:, bass.ds(b * TPB, TPB), :]).then_inc(done, 16)

            load_block(x_next, 0, x_next_in)
            tileno_at = slice(*CONST["tileno"])
            sp.dma_start(cst[:, P:tileno_at.start], consts[:, P:tileno_at.start]).then_inc(const_loaded, 16)
            sp.dma_start(cst[0:1, tileno_at], consts[0:1, tileno_at]).then_inc(const_loaded, 16)
            sp.dma_start(raw_gate.rearrange("p (c n) -> p c n", c=NC), sh_gate.rearrange("(c p) n -> p c n", p=P)).then_inc(raw_loaded, 16)
            sp.dma_start(raw_up.rearrange("p (c n) -> p c n", c=NC), sh_up.rearrange("(c p) n -> p c n", p=P)).then_inc(raw_loaded, 16)
            load_block(x_now, 0, x_now_in)
            sp.dma_start(down_s[:, :, :], sh_down.rearrange("(i p) n -> p i n", p=P)).then_inc(raw_loaded, 16)

            with sp.Fori(0, GROUPS) as g:
                for r in range(GB):
                    sp.wait_ge(normed_ready, g * GB + (r + 1))
                    sp.dma_start(tiles_of(expert_rows)[:, bass.ds(g * (GB * TPB) + r * TPB, TPB), :],
                                 ring[r]).then_inc(normed_stored[r], 16)

            sp.wait_ge(z_ready, 1)
            load_block(x_next, 1, x_next_in)

            def load_expert(e):
                at = (e % SLOTS) * WCOLS
                gate, up, down = (experts[:, at + k * NC * I:at + (k + 1) * NC * I] for k in range(3))
                sp.dma_start(gate.rearrange("p (c n) -> p c n", c=NC), gate_w[e].rearrange("(c p) n -> p c n", p=P)).then_inc(w_landed[e], 16)
                sp.dma_start(up.rearrange("p (c n) -> p c n", c=NC), up_w[e].rearrange("(c p) n -> p c n", p=P)).then_inc(w_landed[e], 16)
                sp.dma_start(down.rearrange("p (i n) -> p i n", i=NI), down_w[e].rearrange("(i p) n -> p i n", p=P)).then_inc(w_landed[e], 16)

            def tell_loaded(e):
                sp.wait_ge(w_landed[e], 48)
                sp.sem_inc(w_loaded, 1)

            sp.wait_ge(map_ready, 1)
            sp.wait_ge(turned_w, 4)
            sp.wait_ge(gu_lo_ready, 2)
            for e in range(SLOTS):
                load_expert(e)
            for e in range(SLOTS):
                tell_loaded(e)

            def body(b, first, last):
                if not first:
                    sp.wait_ge(rest_done, 2 * b)
                    sp.dma_start(tiles_of(rest_rows)[:, bass.ds((b - 1) * TPB, TPB), :], rest[:, :, :]).then_inc(rest_stored, 16)
                if not last:
                    sp.wait_ge(base_ready, b + 1)
                    load_block(x_now, b + 1, x_now_in)
                    if not isinstance(b, int) or b < NB - 2:
                        sp.wait_ge(z_ready, b + 2)
                        load_block(x_next, b + 2, x_next_in)

            body(0, True, False)
            with sp.Fori(1, NB - 2) as b:
                body(b, False, False)
            body(NB - 2, False, False)
            body(NB - 1, False, True)
            sp.wait_ge(rest_done, 2 * NB)
            sp.dma_start(tiles_of(rest_rows)[:, N // P - TPB:N // P, :], rest[:, :, :]).then_inc(rest_stored, 16)
            for e in range(SLOTS, E):
                done = sp.value_load(tiles_upto[0:1, e - SLOTS:e - SLOTS + 1], min_val=1, max_val=ST)
                sp.wait_ge(y_ps, done)
                load_expert(e)
                tell_loaded(e)
            sp.wait_ge(rest_stored, 16 * NB)

        @block.gpsimd
        def _(pool):
            pool.memset(terms[:, :, :, 0:1], 0.0)
            pool.memset(acc[:, :], 0.0)
            pool.memset(stats[:, NB * TPB * NS:], 0.0).then_inc(zero_set, 1)
            entries = sorted_entry[:, :].rearrange("p (t c) -> p t c", c=2)
            pool.memset(entries[:, :, 0:1], N)
            pool.memset(entries[:, :, 1:2], 0)
            pool.memset(prod[:, :], 0.0).then_inc(zero_set, 1)
            pool.iota(entry[:, :].rearrange("p (t c) -> p t c", c=2)[:, :, 0:1], [[P, NT], [0, 1]], base=0,
                      channel_multiplier=1).then_inc(zero_set, 1)
            kb, qb = (const(n).rearrange("p (j m h) -> p j m h", j=TPU, m=M) for n in ("kbias", "qbias"))
            for m in range(M):
                shift = -DH if m in (1, 3) else 0
                pool.memset(kb[:, :, m, :], float(shift))
                pool.memset(qb[:, :, m, :], float(np.float32(shift * BETA[m] * SCALE)))
            for name, v in (("mhalf", -0.5), ("mfive8", -0.625), ("s4bias", -0.5 * A4 ** 0.5), ("r5bias", -0.625 * A5 ** 0.5),
                            ("ones", 1.0)):
                pool.memset(const(name), v)
            for e in range(E):
                a = CONST["rank"][0] + e * NT
                pool.memset(cst[:, a:a + NT], float(E - e))
            for name in ("restart", "keep", "tilemask"):
                pool.memset(const(name), 1.0).then_inc(const_set, 1)
            pool.wait_ge(const_set, 3)
            for name, every in (("restart", UNIT + 1), ("keep", NB // B), ("tilemask", NT)):
                a, z_ = CONST[name]
                for at in range(a, z_, every):
                    ins = pool.memset(cst[:, at:at + 1], 0.0)
            ins.then_inc(const_set, 1)
            pool.wait_ge(zero_set, 3)
            pool.dma_start(table.rearrange("(t p) c -> p t c", p=P), entries).then_inc(pads_stored, 16)
            for rows in (expert_rows, rest_rows):
                for c in range(NC):
                    pool.dma_start(rows[N:N + 1, c * P:(c + 1) * P], zero_row[:, 0:P]).then_inc(pads_stored, 16)

            POOL_STEPS = 4

            def features(u, n0, names, ready, last_ps, done, waits):
                uname, yname, sname, rname = names
                for w in waits:
                    pool.wait_ge(w, u + 1)
                pool.wait_ge(last_ps, u)
                steady(pool)
                k = list(FS)
                at = k.index(uname)
                outs = [FS[k[at + f]] for f in range(M)]
                pool.tensor_tensor(W["uy"], W[uname], W[yname], ALU.mult)
                pool.tensor_tensor(W["ur"], W[uname], W[rname], ALU.mult).then_inc(pool_step, 1)
                for out_, src in zip(outs[0:3], (uname, yname, sname)):
                    pool.tensor_tensor(out_, W[src][:, 0:UNIT], W[src][:, UNIT:BLK], ALU.add)
                pool.wait_ge(pool_step, POOL_STEPS * u + n0 + 1)
                steady(pool)
                pool.tensor_tensor(outs[3], W["uy"][:, 0:UNIT], W["uy"][:, UNIT:BLK], ALU.add)
                pool.tensor_tensor(outs[4], W["ur"][:, 0:UNIT], W["ur"][:, UNIT:BLK], ALU.add).then_inc(done, 1)
                pool.wait_ge(done, u + 1)
                pool.sem_inc(pool_step, 1)

            def k_features(u):
                features(u, 0, ("uk", "yk", "sk", "rk"), kfeat_ready, ksum_ps, kfeat_ready, (uk_ready, rk_ready))

            def q_features(u):
                features(u, 2, ("uq", "yq3", "sq", "rq"), qfeat_ready, qsum_ps, qfeat_ready, (uq_ready, rq_ready))

            def low(b, k, fill, lo, hi, done):
                pool.wait_ge(pT_used, 4 * b + fill + 1)
                steady(pool)
                pool.tensor_tensor(lo[:, k, :], xT_raw[:, k, :], hi[:, k, :].bitcast(F32), ALU.subtract).then_inc(done, 1)

            def low_xn(b):
                for k in range(NC):
                    low(b, k, k, xnT_lo, xnT_hi, xnT_lo_ready)

            def low_xf(b):
                for k in range(NC):
                    low(b, k, NC + k, xfT_lo, xfT_hi, xfT_lo_ready)

            def copy_stats(b, first=False):
                if not first:
                    pool.wait_ge(base_ready, b)
                pool.tensor_copy(stats_now[:, :], stats[:, bass.ds(b * (TPB * NS), 2 * TPB * NS)]).then_inc(now_copied, 1)

            def store_entries(b):
                pool.wait_ge(entries_stored, 16 * TPB * b)
                steady(pool)
                pool.tensor_copy(place_now[:, :], place[:, bass.ds(b * TPB, TPB)])
                pool.tensor_copy(entry_now[:, :], entry[:, bass.ds(b * TPB * 2, TPB * 2)]).then_inc(entry_copied, 1)
                pool.wait_ge(entry_copied, b + 1)
                steady(pool)
                for j in range(TPB):
                    pool.indirect_dma_start(
                        out=table, out_offset=bass.IndirectOffsetOnAxis(ap=place_now[:, j:j + 1], axis=0),
                        in_=entry_now[:, 2 * j:2 * j + 2], in_offset=None).then_inc(entries_stored, 16)

            def body(b, first, last):
                if not first:
                    copy_stats(b)
                k_features(2 * b)
                q_features(2 * b)
                if not last:
                    low_xn(b + 1)
                k_features(2 * b + 1)
                q_features(2 * b + 1)
                store_entries(b)
                if not last:
                    low_xf(b + 1)

            pool.wait_ge(stats_ready, GROUPS)
            copy_stats(0, True)
            low_xn(0)
            for n, raw in enumerate((raw_gate, raw_up)):
                pool.wait_ge(gu_hi_ready, n + 1)
                at = slice(n * NC * I, (n + 1) * NC * I)
                pool.tensor_tensor(gu_lo[:, at], raw, gu_hi[:, at].bitcast(F32), ALU.subtract).then_inc(gu_lo_ready, 1)

            low_xf(0)
            for r in range(GB):
                pool.wait_ge(normed_stored[r], 16 * GROUPS)
            pool.wait_ge(pads_stored, 80)
            pool.wait_ge(score_ready, 1)
            pool.wait_ge(place_ready, 1)
            body(0, True, False)
            with pool.Fori(1, NB - 1) as b:
                body(b, False, False)
            body(NB - 1, False, True)

            pool.wait_ge(entries_stored, 16 * NT)
            pool.dma_start(entries, table.rearrange("(t p) c -> p t c", p=P)).then_inc(entries_back, 16)
            for r in range(GB):
                pool.wait_ge(normed_stored[r], 16 * GROUPS)
            pool.wait_ge(quot_ready, 2 * NB)
            pool.wait_ge(entries_back, 16)

            def seat(into, set_, t, h):
                pool.tensor_copy(into[:, h:h + 1], sorted_entry[:, bass.ds(2 * t, 1)]).then_inc(set_, 1)

            def gather_row(t, i, h):
                seat(seat_x, seat_x_set, t, h)
                pool.wait_ge(seat_x_set, t + 1)
                steady(pool)
                pool.indirect_dma_start(out=e_rows[h], out_offset=None, in_=expert_rows,
                                        in_offset=bass.IndirectOffsetOnAxis(ap=seat_x[:, h:h + 1], axis=0)).then_inc(row_in[h], 16)

            def gather_rest(t, i, h):
                seat(seat_r, seat_r_set, t, h)
                pool.wait_ge(seat_r_set, t + 1)
                steady(pool)
                pool.indirect_dma_start(out=e_rest[h], out_offset=None, in_=rest_rows,
                                        in_offset=bass.IndirectOffsetOnAxis(ap=seat_r[:, h:h + 1], axis=0)).then_inc(rest_in[h], 16)

            def tile(t, i, h, rows_ahead=True, rest_ahead=True):
                if rows_ahead:
                    pool.wait_ge(xT_ps, t + 2)
                    pool.wait_ge(row_in[1 - h], 16 * (i + h) + 16)
                    steady(pool)
                    gather_row(t + 3, i + 1 + h, 1 - h)
                pool.wait_ge(out_stored[h], 16 * i)
                steady(pool)
                seat(seat_o, seat_o_set, t, h)
                pool.wait_ge(seat_o_set, t + 1)
                pool.wait_ge(y_ready, t + 1)
                steady(pool)
                pool.indirect_dma_start(out=out_rows, out_offset=bass.IndirectOffsetOnAxis(ap=seat_o[:, h:h + 1], axis=0),
                                        in_=e_y[h], in_offset=None, bounds_check=N - 1, oob_is_err=False).then_inc(out_stored[h], 16)
                if rest_ahead:
                    pool.wait_ge(rest_in[h], 16 * i + 16)
                    steady(pool)
                    gather_rest(t + 2, i + 1, h)

            gather_row(0, 0, 0)
            gather_row(1, 0, 1)
            pool.wait_ge(rest_stored, 16 * NB)
            gather_rest(0, 0, 0)
            gather_rest(1, 0, 1)
            pool.wait_ge(xT_ps, 1)
            pool.wait_ge(row_in[0], 16)
            gather_row(2, 1, 0)
            with pool.Fori(0, PAIRS) as i:
                tile(2 * i, i, 0)
                tile(2 * i + 1, i, 1)
            tile(ST - 3, PAIRS, 0, False, True)
            tile(ST - 2, PAIRS, 1, False, False)
            tile(ST - 1, PAIRS + 1, 0, False, False)
            pool.wait_ge(out_stored[0], 16 * (PAIRS + 2))
            pool.wait_ge(out_stored[1], 16 * (PAIRS + 1))

        @block.scalar
        def _(act):
            def roots(g):
                at = slice(g * GB * TPB, (g + 1) * GB * TPB)
                act.wait_ge(var_ready, g + 1)
                act.activation(small[:, 2:4, at], small[:, 0:2, at], ACT.Sqrt).then_inc(root_ready, 1)

            def affine(out_, ps, c):
                return act.activation(out_, ps, ACT.Identity, scale=ln_scale[:, c:c + 1], bias=ln_shift[:, c:c + 1])

            def keep_zT(b):
                act.wait_ge(turned, b + 1)
                if b >= 2:
                    act.wait_ge(logT_ps, b - 1)
                for c, ps in enumerate(((pK, pV), (pQ, pG))[b % 2]):
                    ins = affine(flat(ring_T[b % 2][:, :, :])[:, c * BLK:(c + 1) * BLK], ps[:, :], c)
                ins.then_inc(zT_ready, 1)

            def keep_logT(b):
                act.wait_ge(logT_ps, b + 1)
                act.wait_ge(logit_ps, b)
                act.activation(logT, pS[0:E, :], ACT.Copy).then_inc(logT_ready, 1)

            def keep_logits(b):
                act.wait_ge(logit_ps, b + 1)
                act.activation(logit[:, :, b * TPB:(b + 1) * TPB],
                               pR[:, 0:TPB * E].rearrange("p (j e) -> p e j", e=E), ACT.Copy).then_inc(logit_ready, 1)

            roots(0)
            act.wait_ge(first_loaded, FIRSTS)
            for b in range(NB):
                if b == 2:
                    roots(1)
                keep_zT(b)
                if b:
                    keep_logT(b - 1)
                if b > 1:
                    keep_logits(b - 2)
            keep_logT(NB - 1)
            keep_logits(NB - 2)
            keep_logits(NB - 1)

            for s in range(3):
                act.wait_ge(turned_w, s + 1)
                act.activation(win_hi[:, :, s, :], pair((pK, pV, pQ)[s][:, :]), ACT.Copy).then_inc(whi_ready, 1)
            act.wait_ge(turned_w, 4)
            act.activation(wout[:, :, :], pair(pU[:, :]), ACT.Copy).then_inc(wout_ready, 1)
            act.wait_ge(const_set, 4)

            def normed(b, out_, k, done):
                for j in range(TPB):
                    at = (TPB + j) * NS + k
                    ins = act.activation(out_[:, j, :], x_next[:, j, :], ACT.Identity,
                                         scale=stats_now[:, at:at + 1], bias=stats_now[:, at + 1:at + 2])
                ins.then_inc(done, 1)

            def norm_next(b):
                act.wait_ge(x_next_in, 16 * b + 16)
                act.wait_ge(now_copied, b)
                act.wait_ge(pT_ps, 4 * b)
                steady(act)
                normed(b, xn, 0, xn_ready)
                normed(b, z, 2, z_ready)

            def set_base(b, first):
                act.wait_ge(x_now_in, 16 * b + 16)
                act.wait_ge(now_copied, b + 1)
                if not first:
                    act.wait_ge(rest_done, 2 * b)
                    steady(act)
                for j in range(TPB):
                    at = j * NS
                    ins = act.activation(base[:, j, :], x_now[:, j, :], ACT.Identity,
                                         scale=stats_now[:, at + 4:at + 5], bias=stats_now[:, at + 1:at + 2])
                ins.then_inc(base_ready, 1)

            def keep_xn(b, k):
                act.wait_ge(pT_ps, 4 * b + k + 1)
                if not isinstance(b, int) or b:
                    act.wait_ge(xfT_lo_ready, 2 * b + (k - 1))
                    act.wait_ge(v_ps, 2 * b)
                    steady(act)
                act.activation(xT_raw[:, k, :], pT[:, :], ACT.Copy)
                act.activation(xnT_hi[:, k, :], pT[:, :], ACT.Copy).then_inc(pT_used, 1)

            def keep_xf(b, k):
                act.wait_ge(pT_ps, 4 * b + NC + k + 1)
                act.wait_ge(xnT_lo_ready, 2 * b + k + 1)
                act.wait_ge(u_ps, NI * b)
                steady(act)
                affine(xT_raw[:, k, :], pT[:, :], k)
                affine(xfT_hi[:, k, :], pT[:, :], k).then_inc(pT_used, 1)

            def keep_kq(u):
                for ps, have, used, name, done in ((pK, k_ps, uk_ready, "kraw", kraw_ready), (pQ, q_ps, uq_ready, "qraw", qraw_ready)):
                    act.wait_ge(have, u + 1)
                    act.wait_ge(used, u)
                    steady(act)
                    act.activation(W[name], ps[:, :], ACT.Copy).then_inc(done, 1)

            def k_squares(u):
                act.wait_ge(uk_ready, u + 1)
                steady(act)
                act.activation(W["yk"], W["uk"], ACT.Square, scale=0.25).then_inc(yk_ready, 1)
                act.wait_ge(yk_ready, u + 1)
                steady(act)
                act.activation(W["sk"], W["yk"], ACT.Square, bias=const("mhalf")).then_inc(sk_ready, 1)
                act.activation(W["rk"], W["yk"], ACT.Square, bias=const("mfive8")).then_inc(rk_ready, 1)

            def q_squares(u):
                act.wait_ge(uq_ready, u + 1)
                steady(act)
                act.activation(W["yq3"], W["uq"], ACT.Square, scale=0.25 * A3 ** 0.5).then_inc(yq3_ready, 1)
                act.activation(W["yq2"], W["uq"], ACT.Square, scale=0.25 * A2 ** 0.5).then_inc(yq2_ready, 1)
                act.wait_ge(yq3_ready, u + 1)
                steady(act)
                act.activation(W["rq"], W["yq3"], ACT.Square, bias=const("r5bias"), scale=A5 ** 0.5 / A3)
                act.activation(W["sq"], W["yq3"], ACT.Square, bias=const("s4bias"), scale=A4 ** 0.5 / A3).then_inc(rq_ready, 1)

            def widen(u):
                act.wait_ge(recip_ready, u + 1)
                act.wait_ge(spread_ps, u)
                steady(act)
                act.activation(recip_wide[:, :, :], recip[:, :].unsqueeze(2).to_broadcast([P, TPU * HEADS, HG]),
                               ACT.Copy).then_inc(wide_ready, 1)

            def gate(b, n):
                act.wait_ge(g_ps, NI * b + n + 1)
                act.wait_ge(hid_ready, NI * b + n)
                steady(act)
                act.activation(silu[:, :], pG[:, :], ACT.Silu).then_inc(silu_ready, 1)

            def body(b, first, last):
                k_squares(2 * b)
                if not first:
                    widen(2 * b - 1)
                q_squares(2 * b)
                if not last:
                    norm_next(b + 1)
                keep_kq(2 * b + 1)
                set_base(b, first)
                if not last:
                    keep_xn(b + 1, 0)
                gate(b, 0)
                if not last:
                    keep_xn(b + 1, 1)
                k_squares(2 * b + 1)
                gate(b, 1)
                q_squares(2 * b + 1)
                widen(2 * b)
                if not last:
                    keep_kq(2 * b + 2)
                gate(b, 2)
                gate(b, 3)
                if not last:
                    keep_xf(b + 1, 0)
                    keep_xf(b + 1, 1)

            act.wait_ge(x_next_in, 16)
            act.wait_ge(now_copied, 1)

            def first_block(out_, k, done):
                for j in range(TPB):
                    at = j * NS + k
                    ins = act.activation(out_[:, j, :], x_next[:, j, :], ACT.Identity,
                                         scale=stats_now[:, at:at + 1], bias=stats_now[:, at + 1:at + 2])
                ins.then_inc(done, 1)

            first_block(xn, 0, xn_ready)
            keep_xn(0, 0)
            keep_xn(0, 1)
            keep_kq(0)
            first_block(z, 2, z_ready)
            act.wait_ge(raw_loaded, RAWS)
            for n, raw in enumerate((raw_gate, raw_up)):
                act.activation(gu_hi[:, n * NC * I:(n + 1) * NC * I], raw, ACT.Copy).then_inc(gu_hi_ready, 1)
            keep_xf(0, 0)
            keep_xf(0, 1)
            act.wait_ge(best_ready, 1)
            act.wait_ge(zero_set, 3)
            act.activation(entry[:, :].bitcast(F32).rearrange("p (t c) -> p t c", c=2)[:, :, 1:2], best.unsqueeze(2),
                           ACT.Sigmoid).then_inc(score_ready, 1)
            body(0, True, False)
            with act.Fori(1, NB - 1) as b:
                body(b, False, False)
            body(NB - 1, False, True)
            widen(2 * NB - 1)

            act.wait_ge(quot_ready, 2 * NB)
            act.wait_ge(entries_back, 16)
            score = sorted_entry[:, :].bitcast(F32)

            def keep_xT(t, i, h):
                act.wait_ge(xT_ps, t + 1)
                act.wait_ge(eu_ps[h], i)
                steady(act)
                for c in range(NC):
                    ins = affine(e_xT[h][:, c * P:(c + 1) * P], pT[:, c * P:(c + 1) * P], c)
                ins.then_inc(xT_ready, 1)

            def expert_gate(t, h):
                act.wait_ge(eg_ps, t + 1)
                act.wait_ge(ehid_ready, t)
                act.activation(e_silu, e_gate[h][:, :], ACT.Silu, scale=score[:, bass.ds(2 * t + 1, 1)]).then_inc(esilu_ready, 1)

            def keep_hT(t):
                act.wait_ge(hT_ps, t + 1)
                act.wait_ge(y_ps, t)
                steady(act)
                act.activation(e_hT, pQ[:, :], ACT.Copy).then_inc(hT_ready, 1)

            keep_xT(0, 0, 0)
            expert_gate(0, 0)
            keep_xT(1, 0, 1)
            with act.Fori(0, PAIRS) as i:
                expert_gate(2 * i + 1, 1)
                keep_hT(2 * i)
                keep_xT(2 * i + 2, i + 1, 0)
                expert_gate(2 * i + 2, 0)
                keep_hT(2 * i + 1)
                keep_xT(2 * i + 3, i + 1, 1)
            expert_gate(ST - 2, 1)
            keep_hT(ST - 3)
            keep_xT(ST - 1, PAIRS + 1, 0)
            expert_gate(ST - 1, 0)
            keep_hT(ST - 2)
            keep_hT(ST - 1)

        @block.vector
        def _(dve):
            steps = [0]

            def stat_op(ins):
                steps[0] += 1
                ins.then_inc(stat_step, 1)
                dve.wait_ge(stat_step, steps[0])

            for g in range(GROUPS):
                at = slice(g * GB * TPB, (g + 1) * GB * TPB)
                tiles = range(at.start, at.stop)
                for t in tiles:
                    if t % TPB == 0:
                        dve.wait_ge(x_loaded[t // TPB], 16)
                    ins = dve.bn_stats(moments6[:, t, :], x_all[:, t, :])
                stat_op(ins)
                for t in tiles:
                    ins = dve.bn_aggr(moments[:, t, :], moments6[:, t, :])
                stat_op(ins)
                mean, var = moments[:, at, 0], moments[:, at, 1]
                v, root, guess, t0, t1 = (small[:, 2 * k:2 * k + 2, at] for k in range(5))
                both_rstd = stat[:, at, 0:3:2].rearrange("p t k -> p k t")
                stat_op(dve.tensor_scalar(v[:, 0, :], var, LN_EPS, None, ALU.add))
                dve.scalar_tensor_tensor(v[:, 1, :], v[:, 0, :], LN_EPS, v[:, 0, :], ALU.mult, ALU.add).then_inc(var_ready, 1)
                dve.wait_ge(var_ready, g + 1)
                dve.wait_ge(root_ready, g + 1)
                stat_op(dve.reciprocal(guess, root))
                stat_op(dve.tensor_tensor(t0, guess, guess, ALU.mult))
                stat_op(dve.tensor_tensor(t1, t0, v, ALU.mult))
                stat_op(dve.tensor_scalar(t0, t1, -0.5, 1.5, ALU.mult, ALU.add))
                stat_op(dve.tensor_tensor(both_rstd, guess, t0, ALU.mult))
                for b in range(g * GB, (g + 1) * GB):
                    r = b % GB
                    if g:
                        dve.wait_ge(normed_stored[r], 16 * g)
                        dve.wait_ge(turned, b - GB + 1)
                    for j in range(TPB):
                        t = TPB * b + j
                        ins = dve.tensor_scalar(ring[r][:, j, :], x_all[:, t, :], moments[:, t, 0:1], stat[:, t, 2:3],
                                                ALU.subtract, ALU.mult)
                    ins.then_inc(normed_ready, 1)
                for k, s in ((1, 0), (3, 2)):
                    dve.scalar_tensor_tensor(stat[:, at, k], mean, -1.0, stat[:, at, s], ALU.mult, ALU.mult)
                dve.tensor_scalar(stat[:, at, 4], stat[:, at, 0], 1.0, None, ALU.add).then_inc(stats_ready, 1)

            dve.wait_ge(in_loaded, INS)
            for r in range(2):
                ins = dve.tensor_copy(raw_out_c[:, r, :].rearrange("p (c h g) -> p c h g", c=NC, g=HG),
                                      raw_out[:, r, :].rearrange("p (h c g) -> p c h g", c=NC, g=HG))
            ins.then_inc(out_sorted, 1)

            rsteps = [0]

            def route_op(ins):
                rsteps[0] += 1
                ins.then_inc(route_step, 1)
                dve.wait_ge(route_step, rsteps[0])

            def by_tile(ap):
                return ap.rearrange("p e t -> p t e")

            equal, ranked, onehot, upto, where, sums = (grids[:, k, :].rearrange("p (e t) -> p e t", e=E) for k in range(6))
            first = hid[:, 1, 64:64 + NT]
            seats_f = hid[:, 1, 96:96 + NT]
            tiles_i = hid[:, 1, 128:128 + E].bitcast(I32)
            tiles_f, starts = (hid[:, 1, 136 + 8 * k:144 + 8 * k] for k in range(2))
            ends = expert_ends[:, :]
            past = grids[0:1, 0:2, :].rearrange("p a b -> p (a b)")[:, 0:E * ST].rearrange("p (e t) -> p e t", e=E)
            expert, wrap, column = (grids[0:1, 3, 64 * k:64 * k + ST] for k in range(3))
            dve.wait_ge(logit_ready, NB)
            dve.wait_ge(const_loaded, CONSTS)
            dve.wait_ge(const_set, 4)
            dve.tensor_reduce(best, by_tile(logit[:, :, :]), AX, ALU.max).then_inc(best_ready, 1)
            dve.wait_ge(best_ready, 1)
            route_op(dve.tensor_tensor(equal, logit[:, :, :], best[:, None, :].to_broadcast([P, E, NT]), ALU.is_equal))
            route_op(dve.tensor_tensor(ranked, equal, const("rank").rearrange("p (e t) -> p e t", e=E), ALU.mult))
            route_op(dve.tensor_reduce(first, by_tile(ranked), AX, ALU.max))
            dve.tensor_tensor(onehot, ranked, first[:, None, :].to_broadcast([P, E, NT]), ALU.is_equal).then_inc(onehot_ready, 1)
            for s in range(3):
                dve.wait_ge(whi_ready, s + 1)
                dve.tensor_tensor(win_lo[:, :, s, :], pair((pK, pV, pQ)[s][:, :]), win_hi[:, :, s, :].bitcast(F32),
                                  ALU.subtract).then_inc(wlo_ready, 1)
            dve.wait_ge(before_ps, 1)
            flat_upto, flat_sums = upto.rearrange("p e t -> p (e t)"), sums.rearrange("p e t -> p (e t)")
            route_op(dve.tensor_tensor_scan(flat_upto, const("tilemask"), pR[:, 0:E * NT], 0.0, ALU.mult, ALU.add))
            route_op(dve.tensor_tensor(flat_sums, flat_upto, pR[:, 0:E * NT], ALU.subtract))
            route_op(dve.tensor_tensor(where.rearrange("p e t -> p (e t)"), flat_sums, pS[:, 0:E * NT], ALU.add))
            route_op(dve.tensor_scalar(tiles_i, upto[:, :, NT - 1], float(P - 1), None, ALU.add))
            route_op(dve.tensor_scalar(tiles_i, tiles_i, P.bit_length() - 1, None, ALU.arith_shift_right))
            route_op(dve.tensor_scalar(tiles_f, tiles_i, 1.0, None, ALU.max))
            route_op(dve.tensor_tensor_scan(ends, tiles_f, tiles_f, 0.0, ALU.add, ALU.bypass))
            route_op(dve.tensor_tensor(starts, ends, tiles_f, ALU.subtract))
            route_op(dve.tensor_scalar(starts, starts, float(P), None, ALU.mult))
            route_op(dve.tensor_tensor(sums, where, starts.unsqueeze(2).to_broadcast([P, E, NT]), ALU.add))
            route_op(dve.tensor_tensor(where, sums, onehot, ALU.mult))
            route_op(dve.tensor_reduce(seats_f, by_tile(where), AX, ALU.add))
            dve.tensor_copy(place[:, :], seats_f).then_inc(place_ready, 1)
            DEN_STEPS = 5

            def sums_of_k(u, b, first):
                dve.wait_ge(ksum_ps, u + 1)
                dve.wait_ge(prefix_ps, u)
                dve.tensor_tensor(ksb[:, :], ksum_at, const("kbias"), ALU.add).then_inc(den_step, 1)
                dve.wait_ge(den_step, DEN_STEPS * u + 1)
                if not first:
                    dve.wait_ge(acc_kept, b)
                dve.tensor_tensor(acc[:, R:2 * R], acc[:, 0:R], ksb[:, 0:R], ALU.add).then_inc(ksb_ready, 1)

            def denominator(u, b, keep):
                dve.wait_ge(qsum_ps, u + 1)
                dve.tensor_tensor(qsb[:, :], qsum_at, const("qbias"), ALU.add).then_inc(qsb_ready, 1)
                dve.wait_ge(prefix_ps, u + 1)
                dve.tensor_tensor(acc[:, 0:R], acc[:, R:2 * R], ksb[:, R:2 * R], ALU.add).then_inc(den_step, 1)
                dve.wait_ge(qsb_ready, u + 1)
                dve.tensor_tensor(prod[:, :], qsb[:, :], prefix_at, ALU.mult).then_inc(den_step, 1)
                dve.wait_ge(den_step, DEN_STEPS * u + 3)
                if keep:
                    dve.tensor_scalar(acc[:, 0:R], acc[:, 0:R], KEEP(b), None, ALU.mult).then_inc(acc_kept, 1)
                dve.wait_ge(recip_ready, u)
                dve.tensor_reduce(den[:, :], prod[:, :].rearrange("p (j m h) -> p j h m", j=TPU, m=M), AX,
                                  ALU.add).then_inc(den_step, 1)
                dve.wait_ge(den_step, DEN_STEPS * u + 4)
                dve.tensor_scalar(den[:, :], den[:, :], DEN_EPS, None, ALU.add).then_inc(den_step, 1)
                dve.wait_ge(den_step, DEN_STEPS * u + 5)
                dve.wait_ge(wide_ready, u)
                dve.reciprocal(recip[:, :], den[:, :]).then_inc(recip_ready, 1)

            def quotient(u, a):
                dve.wait_ge(spread_ps, u + 1)
                dve.tensor_tensor(num[:, a], num[:, a], spread_at.unsqueeze(1).to_broadcast([P, NC, UNIT]),
                                  ALU.mult).then_inc(quot_ready, 1)

            def KEEP(b):
                at = CONST["keep"][0] + 1
                return cst[:, bass.ds(b + at, 1)]

            def hidden(b, n):
                dve.wait_ge(silu_ready, NI * b + n + 1)
                dve.wait_ge(u_ps, NI * b + n + 1)
                dve.wait_ge(out_ps, 2 * b)
                dve.tensor_tensor(hid[:, n, :], silu[:, :], pU[:, :], ALU.mult).then_inc(hid_ready, 1)

            def add_rest(b):
                dve.wait_ge(base_ready, b + 1)
                dve.wait_ge(rest_stored, 16 * b)
                for k, ps in enumerate((pG, pU)):
                    dve.wait_ge(out_ps, 2 * b + k + 1)
                    dve.tensor_tensor(flat(rest[:, 2 * k:2 * k + 2, :]), flat(base[:, 2 * k:2 * k + 2, :]), ps[:, :],
                                      ALU.add).then_inc(rest_done, 1)

            count = [0]
            UNIT_STEPS = 19

            def unit(b, a, first):
                u = 2 * b + a
                count[0] = 0

                def step(ins):
                    ins.then_inc(dve_step, 1)
                    count[0] += 1
                    return count[0]

                def need(k):
                    dve.wait_ge(dve_step, UNIT_STEPS * u + k)

                def term(m):
                    return terms[:, m, :, 1:UNIT + 1]

                def sum_(m):
                    return run[:, m, :, 1:UNIT + 1]

                def running(m):
                    return step(dve.tensor_tensor_scan(flat(run[:, m]), const("restart"), flat(terms[:, m]), 0.0, ALU.mult, ALU.add))

                uk, yk, sk, rk, uq, yq3, yq2, sq, rq, t1, t2, t3 = (
                    pair(W[n]) for n in ("uk", "yk", "sk", "rk", "uq", "yq3", "yq2", "sq", "rq", "t1", "t2", "t3"))
                v = pair(pV[:, :])
                dve.wait_ge(kraw_ready, u + 1)
                dve.wait_ge(kfeat_ready, u)
                dve.tensor_scalar(W["uk"], W["kraw"], -CLIP, CLIP, ALU.max, ALU.min).then_inc(uk_ready, 1)
                dve.wait_ge(qraw_ready, u + 1)
                dve.wait_ge(qfeat_ready, u)
                dve.tensor_scalar(W["uq"], W["qraw"], -CLIP, CLIP, ALU.max, ALU.min).then_inc(uq_ready, 1)
                dve.wait_ge(v_ps, u + 1)
                dve.wait_ge(uk_ready, u + 1)
                need(0)
                g1 = step(dve.tensor_tensor(term(0), uk, v, ALU.mult))
                dve.wait_ge(yk_ready, u + 1)
                g2 = step(dve.scalar_tensor_tensor(term(1), yk, -0.5, v, ALU.add, ALU.mult))
                need(g1)
                r1 = running(0)
                g3 = step(dve.scalar_tensor_tensor(term(2), yk, -0.75, term(0), ALU.add, ALU.mult))
                need(g2)
                r2 = running(1)
                if a == 1:
                    denominator(u - 1, b, False)
                elif not first:
                    denominator(u - 1, b - 1, True)
                dve.wait_ge(rk_ready, u + 1)
                g4 = dve.scalar_tensor_tensor(term(3), sk, -0.125, v, ALU.add, ALU.mult).then_inc(v_used, 1)
                g5 = step(dve.scalar_tensor_tensor(term(4), rk, -5.0 / 64, term(0), ALU.add, ALU.mult))
                if a == 1:
                    hidden(b, 1)
                need(g3)
                r3 = running(2)
                dve.wait_ge(v_used, u + 1)
                r4 = running(3)
                need(g5)
                r5 = running(4)
                if a == 1 or not first:
                    quotient(u - 1, 1 - a)
                dve.wait_ge(yq3_ready, u + 1)
                need(r3)
                p3 = step(dve.scalar_tensor_tensor(t1, yq3, -0.75 * A3, sum_(2), ALU.add, ALU.mult))
                dve.wait_ge(rq_ready, u + 1)
                need(r5)
                p5 = step(dve.scalar_tensor_tensor(t2, rq, -5.0 / 64 * A5, sum_(4), ALU.add, ALU.mult))
                p2 = step(dve.scalar_tensor_tensor(t3, yq2, -0.5 * A2, sum_(1), ALU.add, ALU.mult))
                need(p5)
                a1 = step(dve.tensor_tensor(t1, t1, t2, ALU.add))
                if a == 0 and not first:
                    add_rest(b - 1)
                if a == 1:
                    hidden(b, 2)
                need(a1)
                p4 = step(dve.scalar_tensor_tensor(t2, sq, -0.125 * A4, sum_(3), ALU.add, ALU.mult))
                a2 = step(dve.tensor_tensor(t1, t1, sum_(0), ALU.add))
                need(p4)
                a3 = step(dve.tensor_tensor(t3, t3, t2, ALU.add))
                need(a2)
                a4 = step(dve.tensor_tensor(t1, t1, uq, ALU.mult))
                if a == 0:
                    sums_of_k(u, b, first)
                else:
                    hidden(b, 3)
                need(a4)
                dve.wait_ge(out_ps, 2 * b)
                numer = step(dve.tensor_tensor(num[:, a], t1, t3, ALU.add))
                if a == 0:
                    step(dve.tensor_copy(terms[:, :, :, 0:1], run[:, :, :, UNIT:UNIT + 1]))
                else:
                    step(dve.tensor_scalar(terms[:, :, :, 0:1], run[:, :, :, UNIT:UNIT + 1], KEEP(b), None, ALU.mult))
                if a == 0:
                    hidden(b, 0)
                else:
                    sums_of_k(u, b, True)
                assert count[0] == UNIT_STEPS, count[0]

            dve.wait_ge(zero_set, 3)
            dve.wait_ge(pads_stored, 80)
            for r in range(GB):
                dve.wait_ge(normed_stored[r], 16 * GROUPS)
            unit(0, 0, True)

            route_op(dve.tensor_tensor(past, const("tileno", 1).rearrange("p (e t) -> p e t", e=E),
                                       ends[0:1, :].unsqueeze(2).to_broadcast([1, E, ST]), ALU.is_ge))
            route_op(dve.tensor_reduce(expert, by_tile(past), AX, ALU.add))
            route_op(dve.tensor_scalar(expert, expert, float(E - 1), None, ALU.min))
            route_op(dve.tensor_copy(column, expert))
            for k in range(SLOTS, E, SLOTS):
                route_op(dve.tensor_scalar(wrap, expert, float(k), -float(SLOTS), ALU.is_ge, ALU.mult))
                route_op(dve.tensor_tensor(column, column, wrap, ALU.add))
            dve.tensor_scalar(tile_at[:, :], column, float(WCOLS), None, ALU.mult)
            dve.tensor_scalar(tile_needs[:, :], expert, 1.0, None, ALU.add)
            dve.tensor_copy(tiles_upto[:, :], ends[0:1, :]).then_inc(map_ready, 1)

            unit(0, 1, True)
            with dve.Fori(1, NB) as b:
                unit(b, 0, False)
                unit(b, 1, False)
            denominator(2 * NB - 1, NB - 1, True)
            quotient(2 * NB - 1, 1)
            add_rest(NB - 1)

            score = sorted_entry[:, :].bitcast(F32)
            dve.wait_ge(entries_back, 16)

            def expert_hidden(t, i, h):
                dve.wait_ge(esilu_ready, t + 1)
                dve.wait_ge(eu_ps[h], i + 1)
                if not isinstance(t, int) or t > 1:
                    dve.wait_ge(hT_ps, t - 1)
                dve.scalar_tensor_tensor(e_hid[h], e_up[h][:, :], score[:, bass.ds(2 * t + 1, 1)], e_silu,
                                         ALU.mult, ALU.mult).then_inc(ehid_ready, 1)

            def expert_out(t, i, h):
                dve.wait_ge(y_ps, t + 1)
                dve.wait_ge(rest_in[h], 16 * i + 16)
                dve.wait_ge(out_stored[h], 16 * i)
                dve.tensor_tensor(e_y[h], e_rest[h], pS[:, 0:D], ALU.add).then_inc(y_ready, 1)

            expert_hidden(0, 0, 0)
            with dve.Fori(0, PAIRS) as i:
                expert_hidden(2 * i + 1, i, 1)
                expert_out(2 * i, i, 0)
                expert_hidden(2 * i + 2, i + 1, 0)
                expert_out(2 * i + 1, i, 1)
            expert_hidden(ST - 2, PAIRS, 1)
            expert_out(ST - 3, PAIRS, 0)
            expert_hidden(ST - 1, PAIRS + 1, 0)
            expert_out(ST - 2, PAIRS, 1)
            expert_out(ST - 1, PAIRS + 1, 0)

        @block.tensor
        def _(pe):
            pe.wait_ge(first_loaded, FIRSTS)

            def turn(b, g, r):
                pe.wait_ge(normed_ready, b + 1)
                if not (isinstance(b, int) and b < 2):
                    pe.wait_ge(zT_ready, b - 1)
                for c, ps in enumerate(((pK, pV), (pQ, pG))[r % 2]):
                    for j in range(TPB):
                        ins = pe.transpose(ps[:, j * P:(j + 1) * P], ring[r][:, j, c * P:(c + 1) * P], ident)
                ins.then_inc(turned, 1)

            def route(b, r):
                zT = flat(ring_T[r % 2][:, :, :])
                pe.wait_ge(zT_ready, b + 1)
                pe.wait_ge(logT_ready, b)
                for c in range(NC):
                    ins = pe.matmul(pS[0:E, :], router[:, c, :], zT[:, c * BLK:(c + 1) * BLK], start=(c == 0), stop=(c == NC - 1))
                ins.then_inc(logT_ps, 1)

            def turn_logits(b):
                pe.wait_ge(logT_ready, b + 1)
                pe.wait_ge(logit_ready, b)
                steady(pe)
                for j in range(TPB):
                    ins = pe.transpose(pR[:, j * E:(j + 1) * E], logT[:, j * P:(j + 1) * P], ident[0:E, 0:E])
                ins.then_inc(logit_ps, 1)

            turn(0, 0, 0)
            turn(1, 0, 1)
            route(0, 0)
            turn(2, 0, 2)
            turn_logits(0)
            route(1, 1)
            turn(3, 0, 3)
            turn_logits(1)
            route(2, 2)
            with pe.Fori(1, GROUPS) as g:
                for r in range(GB):
                    b = g * GB + r
                    turn(b, g, r)
                    turn_logits(b - 2)
                    route(b - 1, (r - 1) % GB)
            turn_logits(NB - 2)
            route(NB - 1, GB - 1)
            turn_logits(NB - 1)

            pe.wait_ge(in_loaded, INS)
            pe.wait_ge(zT_ready, NB)
            for s, ps in enumerate((pK, pV, pQ)):
                for k in range(NC):
                    for c in range(NC):
                        ins = pe.transpose(ps[:, k * D + c * P:k * D + (c + 1) * P], raw_in[:, s, c, k * P:(k + 1) * P], ident)
                ins.then_inc(turned_w, 1)
            pe.wait_ge(out_sorted, 1)
            for c in range(NC):
                for r in range(2):
                    ins = pe.transpose(pU[:, c * D + r * P:c * D + (r + 1) * P], raw_out_c[:, r, c * P:(c + 1) * P], ident)
            ins.then_inc(turned_w, 1)

            pe.wait_ge(onehot_ready, 1)
            pe.wait_ge(const_loaded, CONSTS)
            pe.wait_ge(const_set, 4)
            pe.matmul(pS[:, 0:E * NT], const("before"), grids[:, 2, :], start=True, stop=True)
            pe.matmul(pR[:, 0:E * NT], const("ones"), grids[:, 2, :], start=True, stop=True).then_inc(before_ps, 1)

            def product(ps, terms_):
                n = 3 * len(terms_)
                k = 0
                for lh, ll, rh, rl in terms_:
                    for a, b_ in ((ll, rh), (lh, rl), (lh, rh)):
                        ins = pe.matmul(ps, a, b_, start=(k == 0), stop=(k == n - 1))
                        k += 1
                return ins

            def turn_block(b, k, src, ready, fill):
                pe.wait_ge(ready, b + 1)
                pe.wait_ge(pT_used, 4 * b + fill)
                for j in range(TPB):
                    ins = pe.transpose(pT[:, j * P:(j + 1) * P], src[:, j, k * P:(k + 1) * P], ident)
                ins.then_inc(pT_ps, 1)

            def turn_xn(b, k):
                turn_block(b, k, xn, xn_ready, k)

            def turn_z(b, k):
                turn_block(b, k, z, z_ready, NC + k)

            def project(b, a):
                u = 2 * b + a
                tok = slice(a * UNIT, (a + 1) * UNIT)
                pe.wait_ge(xnT_lo_ready, 2 * b + 2)
                for ps, part, free, done in ((pK, 1, kraw_ready, k_ps), (pQ, 0, qraw_ready, q_ps), (pV, 2, v_used, v_ps)):
                    pe.wait_ge(free, u)
                    for c in range(NC):
                        cols = slice(c * P, (c + 1) * P)
                        ins = product(ps[:, c * UNIT:(c + 1) * UNIT],
                                      [(win_hi[:, k, part, cols], win_lo[:, k, part, cols], xnT_hi[:, k, tok], xnT_lo[:, k, tok])
                                       for k in range(NC)])
                    ins.then_inc(done, 1)

            def gate_up(b, n):
                if n == 0:
                    pe.wait_ge(xfT_lo_ready, 2 * b + 2)
                    pe.wait_ge(rest_done, 2 * b)
                for ps, part, free, done in ((pG, 0, silu_ready, g_ps), (pU, 1, hid_ready, u_ps)):
                    pe.wait_ge(free, NI * b + n)
                    terms_ = []
                    for k in range(NC):
                        at = part * NC * I + k * I + n * P
                        terms_.append((gu_hi[:, at:at + P], gu_lo[:, at:at + P], xfT_hi[:, k, :], xfT_lo[:, k, :]))
                    product(ps[:, :], terms_).then_inc(done, 1)

            def head_sums(u, side):
                names = list(FS)[side * M:(side + 1) * M]
                out_, ready, mat, done = ((ksum_at, kfeat_ready, "ksum", ksum_ps), (qsum_at, qfeat_ready, "qsum", qsum_ps))[side]
                pe.wait_ge(ready, u + 1)
                pe.wait_ge(qsb_ready, u)
                for j in range(TPU):
                    for f, name in enumerate(names):
                        at = CONST[mat][0] + f * R
                        ins = pe.matmul(out_[:, j * R:(j + 1) * R], FS[name][:, j * P:(j + 1) * P], cst[:, at:at + R],
                                        start=(f == 0), stop=(f == M - 1))
                ins.then_inc(done, 1)

            def prefix(u):
                pe.wait_ge(ksb_ready, u + 1)
                pe.wait_ge(quot_ready, u)
                pe.matmul(prefix_at, const("upto"), ksb[:, :], start=True, stop=False)
                pe.matmul(prefix_at, const("ones"), acc[:, :], start=False, stop=True).then_inc(prefix_ps, 1)

            def spread(u):
                pe.wait_ge(wide_ready, u + 1)
                for j in range(TPU):
                    ins = pe.transpose(spread_at[:, j * P:(j + 1) * P], flat(recip_wide[:, j * HEADS:(j + 1) * HEADS, :]), ident)
                ins.then_inc(spread_ps, 1)

            def down_shared(b, k):
                pe.wait_ge(hid_ready, NI * b + NI)
                for j in range(TPU):
                    at = (TPU * k + j) * P
                    for n in range(NI):
                        pe.matmul((pG, pU)[k][:, j * D:(j + 1) * D], hid[:, n, at:at + P], down_s[:, n, :],
                                  start=(j == 0 and n == 0), stop=False, skip_group_check=True)

            def project_out(b):
                pe.wait_ge(quot_ready, 2 * b + 2)
                for k, ps in enumerate((pG, pU)):
                    for j in range(TPU):
                        for c in range(NC):
                            ins = pe.matmul(ps[:, j * D:(j + 1) * D], num[:, k, c, j * P:(j + 1) * P], wout[:, c, :],
                                            start=False, stop=(c == NC - 1), skip_group_check=True)
                    ins.then_inc(out_ps, 1)

            def body(b, first, last):
                if not first:
                    spread(2 * b - 1)
                    down_shared(b - 1, 1)
                project(b, 1)
                if not first:
                    project_out(b - 1)
                head_sums(2 * b, 0)
                if not last:
                    turn_xn(b + 1, 0)
                gate_up(b, 0)
                if not last:
                    turn_xn(b + 1, 1)
                prefix(2 * b)
                head_sums(2 * b, 1)
                gate_up(b, 1)
                if not last:
                    project(b + 1, 0)
                spread(2 * b)
                gate_up(b, 2)
                gate_up(b, 3)
                if not last:
                    turn_z(b + 1, 0)
                head_sums(2 * b + 1, 0)
                if not last:
                    turn_z(b + 1, 1)
                prefix(2 * b + 1)
                head_sums(2 * b + 1, 1)
                down_shared(b, 0)

            pe.wait_ge(wlo_ready, 3)
            turn_xn(0, 0)
            turn_xn(0, 1)
            project(0, 0)
            turn_z(0, 0)
            turn_z(0, 1)
            pe.wait_ge(wout_ready, 1)
            pe.wait_ge(gu_lo_ready, 2)
            body(0, True, False)
            with pe.Fori(1, NB - 1) as b:
                body(b, False, False)
            body(NB - 1, False, True)
            spread(2 * NB - 1)
            down_shared(NB - 1, 1)
            project_out(NB - 1)

            pe.wait_ge(map_ready, 1)
            pe.wait_ge(rest_done, 2 * NB)

            def turn_rows(t, i, h):
                pe.wait_ge(row_in[h], 16 * i + 16)
                pe.wait_ge(xT_ready, t)
                for c in range(NC):
                    ins = pe.transpose(pT[:, c * P:(c + 1) * P], e_rows[h][:, c * P:(c + 1) * P], ident)
                ins.then_inc(xT_ps, 1)

            def up_or_gate(t, h, part, at):
                ps, done = ((e_gate[h], eg_ps), (e_up[h], eu_ps[h]))[part]
                for k in range(NC):
                    ins = pe.matmul(ps[:, :], e_xT[h][:, k * P:(k + 1) * P],
                                    experts[:, bass.ds(at + (part * NC * I + k * I), I)], start=(k == 0), stop=(k == NC - 1))
                ins.then_inc(done, 1)

            def turn_hidden(t, h):
                pe.wait_ge(ehid_ready, t + 1)
                pe.wait_ge(hT_ready, t)
                for n in range(NI):
                    ins = pe.transpose(pQ[:, n * P:(n + 1) * P], e_hid[h][:, n * P:(n + 1) * P], ident)
                ins.then_inc(hT_ps, 1)

            def down(t, at):
                pe.wait_ge(hT_ready, t + 1)
                pe.wait_ge(y_ready, t)
                for n in range(NI):
                    ins = pe.matmul(pS[:, 0:D], e_hT[:, n * P:(n + 1) * P],
                                    experts[:, bass.ds(at + (2 * NC * I + n * D), D)], start=(n == 0), stop=(n == NI - 1))
                ins.then_inc(y_ps, 1)

            def tile(t, i, h, ahead, behind):
                needs = pe.value_load(tile_needs[0:1, bass.ds(t, 1)], min_val=1, max_val=E)
                pe.wait_ge(w_loaded, needs)
                steady(pe)
                at = pe.value_load(tile_at[0:1, bass.ds(t, 1)], min_val=0, max_val=(SLOTS - 1) * WCOLS)
                pe.wait_ge(xT_ready, t + 1)
                up_or_gate(t, h, 0, at)
                if behind:
                    turn_hidden(t - 1, 1 - h)
                up_or_gate(t, h, 1, at)
                if ahead:
                    i1, h1 = (i, 1) if h == 0 else (i + 1, 0)
                    turn_rows(t + 1, i1, h1)
                if behind:
                    before = pe.value_load(tile_at[0:1, bass.ds(t - 1, 1)], min_val=0, max_val=(SLOTS - 1) * WCOLS)
                    down(t - 1, before)

            turn_rows(0, 0, 0)
            tile(0, 0, 0, True, False)
            with pe.Fori(0, PAIRS) as i:
                tile(2 * i + 1, i, 1, True, True)
                tile(2 * i + 2, i + 1, 0, True, True)
            tile(ST - 2, PAIRS, 1, True, True)
            tile(ST - 1, PAIRS + 1, 0, False, True)
            turn_hidden(ST - 1, 0)
            down(ST - 1, pe.value_load(tile_at[0:1, ST - 1:ST], min_val=0, max_val=(SLOTS - 1) * WCOLS))


_INS = ["L0_attn_x", "L0_attn_W_in", "L0_attn_W_out", "L0_ffn_ln_w", "L0_ffn_ln_b", "L0_ffn_router_w", "L0_ffn_gate_w",
        "L0_ffn_up_w", "L0_ffn_down_w", "L0_ffn_sh_gate", "L0_ffn_sh_up", "L0_ffn_sh_down"]


def kernel(**inputs):
    import numpy as _np
    import concourse.bacc as _bacc
    from concourse import mybir as _mybir
    from concourse.bass_utils import run_bass_kernel_spmd as _run

    nc = _bacc.Bacc("TRN2", target_bir_lowering=False, num_devices=1)
    arrays, args = {"constants": constants()}, []
    for name in _INS:
        arrays[name] = _np.ascontiguousarray(inputs[name])
    for name, a in arrays.items():
        args.append(nc.dram_tensor(name, a.shape, _mybir.dt.from_np(a.dtype), kind="ExternalInput").ap())
    out = nc.dram_tensor("out", (B, S, D), _mybir.dt.float32, kind="ExternalOutput").ap()
    token_layer_kernel(nc, *args, out)
    r = _run(nc, [arrays], core_ids=[0])
    return r.results[0]["out"]
```

```python
from contextlib import ExitStack

import numpy as np

import concourse.bass as bass
from concourse import mybir

ALU = mybir.AluOpType
ACT = mybir.ActivationFunctionType
AX = mybir.AxisListType.X
F32 = mybir.dt.float32
F32R = mybir.dt.float32r
I32 = mybir.dt.int32

P = 128
B, S, D = 2, 2048, 256
N = B * S
NT = N // P
BLK = 512
TPB = BLK // P
NB = N // BLK
UNIT = BLK // 2
TPU = UNIT // P
NC = D // P
HEADS = 16
DH = D // HEADS
I = 512
NI = I // P
E = 8
LN_EPS = 1e-5
M = 5
R = M * HEADS
HG = DH // NC
ST = NT + E - 1
PAIRS = (ST - 3) // 2
SLOTS = 2
WCOLS = 2 * NC * I + NI * D


def chebyshev_weights():
    order = 6
    j = np.arange(order, dtype=np.float32)
    alpha = (j + 1.0) ** (-1.5)
    tail = np.flip(np.cumsum(np.flip(alpha)))
    beta = np.concatenate([np.zeros(1, np.float32), tail[1:].astype(np.float32), np.zeros(order - 1, np.float32)])
    return [float(x) for x in (beta / beta.sum())[1:M + 1]]


BETA = chebyshev_weights()
SCALE = 16.0 / BETA[0]
A2, A3 = 4 * BETA[1] * SCALE, BETA[2] * SCALE
A4, A5 = 64 * BETA[3] * SCALE, 16 * BETA[4] * SCALE
DEN_EPS = 1e-7 * SCALE
CLIP = float(np.float32(1.0 - 1e-6)) * 4.0


def layout(*parts):
    at, where = 0, {}
    for name, width in parts:
        where[name] = (at, at + width)
        at += width
    return where, at


CONST, SENT_COLS = layout(
    ("ident", P), ("before", P), ("upto", P), ("ksum", M * R), ("qsum", M * R), ("tileno", E * ST))
SET, CONST_COLS = layout(
    ("sent", SENT_COLS), ("ones", P), ("kbias", TPU * R), ("qbias", TPU * R), ("restart", NC * (UNIT + 1)),
    ("mhalf", 1), ("mfive8", 1), ("s4bias", 1), ("r5bias", 1), ("keep", NB + 1))
CONST.update(SET)


def constants():
    c = np.zeros((P, SENT_COLS), np.float32)

    def put(name, value):
        a, b = CONST[name]
        c[:, a:b] = value.reshape(P, -1)

    put("ident", np.eye(P, dtype=np.float32))
    put("before", np.triu(np.ones((P, P), np.float32), 1))
    put("upto", np.triu(np.ones((P, P), np.float32)))
    feat = np.zeros((2, M, M))
    feat[0, 0, [0, 2, 4]] = 0.25, -0.75, -4 * 5 / 64
    feat[0, 1, 1] = 2.0
    feat[0, 2, 3] = 8.0
    feat[0, 3, 2] = 1.0
    feat[0, 4, 4] = 4.0
    feat[1] = feat[0] * np.array(BETA)[None, :] * SCALE
    feat[1, 1, 1] /= A3
    feat[1, 3, 2] /= A3
    feat[1, 2, 3] /= A4
    feat[1, 4, 4] /= A5
    for side, name in enumerate(("ksum", "qsum")):
        w = np.zeros((P, M, M, HEADS), np.float32)
        for ch in range(P):
            w[ch, :, :, ch // HG] = feat[side]
        put(name, w)
    put("tileno", np.broadcast_to(np.arange(ST, dtype=np.float32)[None, None], (P, E, ST)))
    return c


def token_layer_kernel(nc, consts, x, W_in, W_out, ln_w, ln_b, router_w, gate_w, up_w, down_w,
                       sh_gate, sh_up, sh_down, out):
    with ExitStack() as ctx:
        def sb(name, shape, dt=F32):
            return ctx.enter_context(nc.sbuf_tensor(name, shape, dt))

        def bank(name):
            return ctx.enter_context(nc.psum_tensor(name, [P, BLK], F32))

        def sem(name):
            return ctx.enter_context(nc.semaphore(name))

        x_rows = x.rearrange("b s d -> (b s) d")
        out_rows = out.rearrange("b s d -> (b s) d")
        expert_rows = nc.dram_tensor("expert_rows", [N + 1, D], F32, kind="Internal").ap()
        rest_rows = nc.dram_tensor("rest_rows", [N + 1, D], F32, kind="Internal").ap()
        table = nc.dram_tensor("table", [ST * P, 2], I32, kind="Internal").ap()

        def tiles_of(dram):
            return dram[0:N, :].rearrange("(t p) d -> p t d", p=P)

        cst = sb("cst", [P, CONST_COLS])

        def const(name, part=P):
            a, b = CONST[name]
            return cst[0:part, a:b]

        ident = const("ident")
        router = sb("router", [P, NC, E])
        ln_scale = sb("ln_scale", [P, NC])
        ln_shift = sb("ln_shift", [P, NC])
        rounded = sb("rounded", [P, 2 * SLOTS * WCOLS + 4 * D + 2 * I], F32R)
        rounded_at = [0]

        def view(width):
            rounded_at[0] += width
            return rounded[:, rounded_at[0] - width:rounded_at[0]]

        win_hi, win_lo = [view(3 * NC * D).rearrange("p (k s d) -> p k s d", k=NC, s=3) for _ in range(2)]
        xnT_hi, xnT_lo, xfT_hi, xfT_lo = [view(NC * BLK).rearrange("p (c n) -> p c n", c=NC) for _ in range(4)]
        gu_hi, gu_lo = [view(2 * NC * I) for _ in range(2)]
        wout_hi, wout_lo = [view(NC * D).rearrange("p (c n) -> p c n", c=NC) for _ in range(2)]
        num_hi, num_lo = [view(NC * BLK).rearrange("p (a c n) -> p a c n", a=TPB // TPU, c=NC) for _ in range(2)]
        rounded_at[0] = 2 * SLOTS * WCOLS
        e_xT_hi, e_xT_lo = [[view(D) for _ in range(2)] for _ in range(2)]
        e_hT_hi, e_hT_lo = [view(I) for _ in range(2)]
        down_s = sb("down_s", [P, NI, D])
        experts = sb("experts", [P, SLOTS * WCOLS])
        work = sb("work", [P, 16, BLK])
        terms = sb("terms", [P, M, NC, UNIT + 1])
        run = sb("run", [P, M, NC, UNIT + 1])
        num = sb("num", [P, TPB // TPU, NC, UNIT])
        fsum = sb("fsum", [P, 2 * M, UNIT])
        x_now, x_next, xn, z, base, rest = [sb(n, [P, TPB, D]) for n in ("x_now", "x_next", "xn", "z", "base", "rest")]
        xT_raw = sb("xT_raw", [P, NC, BLK])
        hid = sb("hid", [P, NI, BLK])
        silu = sb("silu", [P, BLK])
        ksb, qsb, acc, prod = [sb(n, [P, TPU * R]) for n in ("ksb", "qsb", "acc", "prod")]
        den = sb("den", [P, TPU * HEADS])
        recip = sb("recip", [P, TPU * HEADS])
        recip_wide = sb("recip_wide", [P, TPU * HEADS, HG])
        NS = 5
        stats = sb("stats", [P, (NB + 1) * TPB * NS])
        stats_now = sb("stats_now", [P, 2 * TPB * NS])
        logit = sb("logit", [P, E, NT])
        expert_ends = sb("expert_ends", [P, E])
        place = sb("place", [P, NT], I32)
        place_now = sb("place_now", [P, TPB], I32)
        entry = sb("entry", [P, NT * 2], I32)
        entry_now = sb("entry_now", [P, TPB * 2], I32)
        sorted_entry = sb("sorted_entry", [P, ST * 2], I32)
        seat_x, seat_r, seat_o = [sb(n, [P, 2], I32) for n in ("seat_x", "seat_r", "seat_o")]
        tile_expert = sb("tile_expert", [1, ST], I32)
        tile_split = sb("tile_split", [1, ST], I32)

        def flat(ap):
            return ap.rearrange("p a b -> p (a b)")

        def pair(ap):
            return ap.rearrange("p (c n) -> p c n", c=NC)

        W = {name: work[:, n, :] for n, name in enumerate(
            ("kraw", "qraw", "uk", "yk", "sk", "rk", "uq", "yq3", "yq2", "sq", "rq", "uy", "ur", "t1", "t2", "t3"))}
        FS = {name: fsum[:, n, :] for n, name in enumerate(
            ("uk", "yk", "sk", "uyk", "urk", "uq", "yq3", "sq", "uyq", "urq"))}

        x_all = flat(work[:, :, :]).rearrange("p (t d) -> p t d", d=D)
        flat_run, flat_fsum = run[:, :, :, :].rearrange("p m c n -> p (m c n)"), flat(fsum[:, :, :])
        ring = [t[:, h * TPB * D:(h + 1) * TPB * D].rearrange("p (t d) -> p t d", d=D) for t in (flat_run, flat_fsum) for h in range(2)]
        logT = hid[0:E, 2, :]
        ring_T = (base, rest)
        raw_gate = experts[:, 0:NC * I]
        raw_up = experts[:, NC * I:2 * NC * I]
        raw_in = experts[:, 2048:2048 + 6 * D].rearrange("p (s c d) -> p s c d", s=3, c=NC)
        raw_out = experts[:, 3584:3584 + 2 * D].rearrange("p (r d) -> p r d", r=2)
        raw_out_c = experts[:, 4096:4096 + 2 * D].rearrange("p (r d) -> p r d", r=2)
        grids = experts[:, 4608:4608 + 6 * E * NT].rearrange("p (k n) -> p k n", k=6)
        moments6 = silu[:, 0:NT * 6].rearrange("p (t s) -> p t s", s=6)
        moments = silu[:, NT * 6:NT * 8].rearrange("p (t s) -> p t s", s=2)
        rank, tilemask = (flat(num[:, k]).rearrange("p (e t) -> p e t", t=NT)[:, 0:E, :] for k in range(2))
        small = hid[:, 0, 0:10 * NT].rearrange("p (k t) -> p k t", t=NT)
        zero_row = prod[0:1, :]
        stat = stats[:, :].rearrange("p (t s) -> p t s", s=NS)
        best = hid[:, 1, 0:NT]

        e_rows = [xn[:, k, :] for k in range(2)]
        e_xT = z[:, 0, :]
        e_rest = [work[:, 2 + k, 0:D] for k in range(2)]
        e_silu = work[:, 6, :]
        e_hid = [work[:, 7 + k, :] for k in range(2)]
        e_y = [work[:, 10 + k, 0:D] for k in range(2)]
        PIECES = 3
        PIECE = WCOLS // PIECES

        pK, pV, pQ, pG, pU, pS, pR, pT = [bank(n) for n in ("pK", "pV", "pQ", "pG", "pU", "pS", "pR", "pT")]
        ksum_at, qsum_at = pS[:, 0:TPU * R], pS[:, TPU * R:2 * TPU * R]
        prefix_at, spread_at = pR[:, 0:TPU * R], pR[:, UNIT:2 * UNIT]
        e_gate, e_up = (pK, pG), (pV, pU)

        x_loaded = [sem(f"x_loaded{b}") for b in range(NB)]
        first_loaded, const_loaded, in_loaded, raw_loaded, down_loaded, const_set, zero_set, pads_stored, passed = [
            sem(n) for n in ("first_loaded", "const_loaded", "in_loaded", "raw_loaded", "down_loaded", "const_set", "zero_set", "pads_stored",
                             "passed")]
        stat_step, var_ready, root_ready, stats_ready = [sem(n) for n in ("stat_step", "var_ready", "root_ready", "stats_ready")]
        normed_ready, turned, zT_ready, logT_ps, logT_ready, logit_ps, logit_ready = [
            sem(n) for n in ("normed_ready", "turned", "zT_ready", "logT_ps", "logT_ready", "logit_ps", "logit_ready")]
        normed_stored = [sem(f"normed_stored{r}") for r in range(4)]
        gu_hi_ready, gu_lo_ready, out_sorted = sem("gu_hi_ready"), sem("gu_lo_ready"), sem("out_sorted")
        turned_w, whi_ready, wlo_ready, wout_hi_ready, wout_lo_ready = [
            sem(n) for n in ("turned_w", "whi_ready", "wlo_ready", "wout_hi_ready", "wout_lo_ready")]
        route_step, onehot_ready, before_ps, best_ready, score_ready, place_ready, map_ready = [
            sem(n) for n in ("route_step", "onehot_ready", "before_ps", "best_ready", "score_ready", "place_ready", "map_ready")]
        x_now_in, x_next_in, now_copied, xn_ready, z_ready, base_ready = [
            sem(n) for n in ("x_now_in", "x_next_in", "now_copied", "xn_ready", "z_ready", "base_ready")]
        entry_copied, entries_stored = sem("entry_copied"), sem("entries_stored")
        pT_ps, pT_used, xnT_lo_ready, xfT_lo_ready = [sem(n) for n in ("pT_ps", "pT_used", "xnT_lo_ready", "xfT_lo_ready")]
        k_ps, v_ps, q_ps, v_used, kraw_ready, qraw_ready = [
            sem(n) for n in ("k_ps", "v_ps", "q_ps", "v_used", "kraw_ready", "qraw_ready")]
        uk_ready, yk_ready, sk_ready, rk_ready = [sem(n) for n in ("uk_ready", "yk_ready", "sk_ready", "rk_ready")]
        uq_ready, yq3_ready, yq2_ready, sq_ready, rq_ready = [
            sem(n) for n in ("uq_ready", "yq3_ready", "yq2_ready", "sq_ready", "rq_ready")]
        pool_step, kfeat_ready, qfeat_ready, ksum_ps, qsum_ps = [
            sem(n) for n in ("pool_step", "kfeat_ready", "qfeat_ready", "ksum_ps", "qsum_ps")]
        den_step, ksb_ready, qsb_ready, acc_kept, prefix_ps, recip_ready, wide_ready, spread_ps, quot_ready = [
            sem(n) for n in ("den_step", "ksb_ready", "qsb_ready", "acc_kept", "prefix_ps", "recip_ready", "wide_ready",
                             "spread_ps", "quot_ready")]
        g_ps, u_ps, silu_ready, hid_ready = [sem(n) for n in ("g_ps", "u_ps", "silu_ready", "hid_ready")]
        num_hi_ready, num_lo_ready = sem("num_hi_ready"), sem("num_lo_ready")
        out_ps, rest_done, rest_stored, dve_step = sem("out_ps"), sem("rest_done"), sem("rest_stored"), sem("dve_step")
        w_landed = [sem(f"w_landed{e}") for e in range(E)]
        w_loaded, entries_back, seat_x_set, seat_r_set, seat_o_set = [
            sem(n) for n in ("w_loaded", "entries_back", "seat_x_set", "seat_r_set", "seat_o_set")]
        w_high, w_low = sem("w_high"), sem("w_low")
        row_in = [sem(f"row_in{h}") for h in range(2)]
        rest_in = [sem(f"rest_in{h}") for h in range(2)]
        out_stored = [sem(f"out_stored{h}") for h in range(2)]
        eg_ps = sem("eg_ps")
        eu_ps = [sem(f"eu_ps{h}") for h in range(2)]
        xT_ps, xT_kept, xT_hi_ready, xT_lo_ready, esilu_ready, ehid_ready, hT_ps, hT_hi_ready, hT_lo_ready, y_ps, y_ready = [
            sem(n) for n in ("xT_ps", "xT_kept", "xT_hi_ready", "xT_lo_ready", "esilu_ready", "ehid_ready", "hT_ps",
                             "hT_hi_ready", "hT_lo_ready", "y_ps", "y_ready")]

        FIRSTS = 16 * (2 + 2 * NC)
        CONSTS = 16 * 2
        INS = 16 * (3 * NC + 1)
        RAWS = 16 * 2
        GROUPS, GB = 2, 4

        def steady(eng):
            eng.sem_inc(passed, 1)

        def piece(slot, n, part=None):
            if part is None:
                return experts[:, bass.ds(slot * WCOLS + n * PIECE, PIECE)]
            return rounded[:, bass.ds(slot * (2 * WCOLS) + (part * WCOLS + n * PIECE), PIECE)]

        def split_hi(act, slot, n):
            act.activation(piece(slot, n, 0), piece(slot, n), ACT.Copy).then_inc(w_high, 1)

        def split_lo(eng, slot, n):
            eng.tensor_tensor(piece(slot, n, 1), piece(slot, n), piece(slot, n, 0).bitcast(F32), ALU.subtract).then_inc(w_low, 1)

        block = ctx.enter_context(nc.Block())

        @block.sync
        def _(sp):
            for b in range(NB):
                sp.dma_start(x_all[:, TPB * b:TPB * (b + 1), :],
                             tiles_of(x_rows)[:, TPB * b:TPB * (b + 1), :]).then_inc(x_loaded[b], 16)
                if b == 0:
                    sp.dma_start(ident, consts[:, 0:P]).then_inc(first_loaded, 16)
                    sp.dma_start(router[:, :, :], router_w.rearrange("(c p) e -> p c e", p=P)).then_inc(first_loaded, 16)
                    for c in range(NC):
                        sp.dma_start(ln_scale[:, c:c + 1], ln_w[c * P:(c + 1) * P].unsqueeze(1)).then_inc(first_loaded, 16)
                        sp.dma_start(ln_shift[:, c:c + 1], ln_b[c * P:(c + 1) * P].unsqueeze(1)).then_inc(first_loaded, 16)
            w_rows = W_in.rearrange("(s h c g) d -> s c h g d", s=3, c=NC, g=HG)
            for s in range(3):
                for c in range(NC):
                    sp.dma_start(raw_in[:, s, c, :], w_rows[s, c]).then_inc(in_loaded, 16)
            sp.dma_start(raw_out, W_out.rearrange("(r p) d -> p r d", p=P)).then_inc(in_loaded, 16)

            def load_block(into, b, done):
                sp.dma_start(into[:, :, :], tiles_of(x_rows)[:, bass.ds(b * TPB, TPB), :]).then_inc(done, 16)

            sp.dma_start(raw_gate.rearrange("p (c n) -> p c n", c=NC), sh_gate.rearrange("(c p) n -> p c n", p=P)).then_inc(raw_loaded, 16)
            sp.dma_start(raw_up.rearrange("p (c n) -> p c n", c=NC), sh_up.rearrange("(c p) n -> p c n", p=P)).then_inc(raw_loaded, 16)
            tileno_at = slice(*CONST["tileno"])
            sp.dma_start(cst[:, P:tileno_at.start], consts[:, P:tileno_at.start]).then_inc(const_loaded, 16)
            sp.dma_start(cst[0:1, tileno_at], consts[0:1, tileno_at]).then_inc(const_loaded, 16)
            with sp.Fori(0, GROUPS) as g:
                for r in range(GB):
                    sp.wait_ge(normed_ready, g * GB + (r + 1))
                    sp.dma_start(tiles_of(expert_rows)[:, bass.ds(g * (GB * TPB) + r * TPB, TPB), :],
                                 ring[r]).then_inc(normed_stored[r], 16)

            sp.dma_start(down_s[:, :, :], sh_down.rearrange("(i p) n -> p i n", p=P)).then_inc(down_loaded, 16)
            load_block(x_now, 0, x_now_in)
            load_block(x_next, 1, x_next_in)


            def load_expert(e):
                at = (e % SLOTS) * WCOLS
                gate, up, down = (experts[:, at + k * NC * I:at + (k + 1) * NC * I] for k in range(3))
                sp.dma_start(gate.rearrange("p (c n) -> p c n", c=NC), gate_w[e].rearrange("(c p) n -> p c n", p=P)).then_inc(w_landed[e], 16)
                sp.dma_start(up.rearrange("p (c n) -> p c n", c=NC), up_w[e].rearrange("(c p) n -> p c n", p=P)).then_inc(w_landed[e], 16)
                sp.dma_start(down.rearrange("p (i n) -> p i n", i=NI), down_w[e].rearrange("(i p) n -> p i n", p=P)).then_inc(w_landed[e], 16)

            def tell_loaded(e):
                sp.wait_ge(w_landed[e], 48)
                sp.sem_inc(w_loaded, 1)

            sp.wait_ge(map_ready, 1)
            sp.wait_ge(turned_w, 4)
            sp.wait_ge(gu_lo_ready, 2)
            for e in range(SLOTS):
                load_expert(e)
            for e in range(SLOTS):
                tell_loaded(e)

            def body(b, first, last):
                if not first:
                    sp.wait_ge(rest_done, 2 * b)
                    sp.dma_start(tiles_of(rest_rows)[:, bass.ds((b - 1) * TPB, TPB), :], rest[:, :, :]).then_inc(rest_stored, 16)
                if not last:
                    sp.wait_ge(base_ready, b + 1)
                    load_block(x_now, b + 1, x_now_in)
                    if not isinstance(b, int) or b < NB - 2:
                        sp.wait_ge(z_ready, b + 2)
                        load_block(x_next, b + 2, x_next_in)

            body(0, True, False)
            with sp.Fori(1, NB - 2) as b:
                body(b, False, False)
            body(NB - 2, False, False)
            body(NB - 1, False, True)
            sp.wait_ge(rest_done, 2 * NB)
            sp.dma_start(tiles_of(rest_rows)[:, N // P - TPB:N // P, :], rest[:, :, :]).then_inc(rest_stored, 16)
            for e in range(SLOTS, E):
                sp.wait_ge(w_low, PIECES * (e - SLOTS + 1))
                load_expert(e)
                tell_loaded(e)
            sp.wait_ge(rest_stored, 16 * NB)

        @block.gpsimd
        def _(pool):
            pool.memset(terms[:, :, :, 0:1], 0.0)
            pool.memset(acc[:, :], 0.0)
            pool.memset(stats[:, NB * TPB * NS:], 0.0).then_inc(zero_set, 1)
            entries = sorted_entry[:, :].rearrange("p (t c) -> p t c", c=2)
            pool.memset(entries[:, :, 0:1], N)
            pool.memset(entries[:, :, 1:2], 0)
            pool.memset(prod[:, :], 0.0).then_inc(zero_set, 1)
            pool.iota(entry[:, :].rearrange("p (t c) -> p t c", c=2)[:, :, 0:1], [[P, NT], [0, 1]], base=0,
                      channel_multiplier=1).then_inc(zero_set, 1)
            kb, qb = (const(n).rearrange("p (j m h) -> p j m h", j=TPU, m=M) for n in ("kbias", "qbias"))
            for m in range(M):
                shift = -DH if m in (1, 3) else 0
                pool.memset(kb[:, :, m, :], float(shift))
                pool.memset(qb[:, :, m, :], float(np.float32(shift * BETA[m] * SCALE)))
            for name, v in (("mhalf", -0.5), ("mfive8", -0.625), ("s4bias", -0.5 * A4 ** 0.5), ("r5bias", -0.625 * A5 ** 0.5),
                            ("ones", 1.0)):
                pool.memset(const(name), v)
            for e in range(E):
                pool.memset(rank[:, e, :], float(E - e))
            for ap in (const("restart"), const("keep"), flat(tilemask)):
                pool.memset(ap, 1.0).then_inc(const_set, 1)
            pool.wait_ge(const_set, 3)
            for name, every in (("restart", UNIT + 1), ("keep", NB // B)):
                a, z_ = CONST[name]
                for at in range(a, z_, every):
                    pool.memset(cst[:, at:at + 1], 0.0)
            ins = pool.memset(tilemask[:, :, 0:1], 0.0)
            ins.then_inc(const_set, 1)
            pool.wait_ge(zero_set, 3)
            pool.dma_start(table.rearrange("(t p) c -> p t c", p=P), entries).then_inc(pads_stored, 16)
            for rows in (expert_rows, rest_rows):
                for c in range(NC):
                    pool.dma_start(rows[N:N + 1, c * P:(c + 1) * P], zero_row[:, 0:P]).then_inc(pads_stored, 16)

            POOL_STEPS = 4

            def features(u, n0, names, ready, last_ps, done, waits):
                uname, yname, sname, rname = names
                for w in waits:
                    pool.wait_ge(w, u + 1)
                pool.wait_ge(last_ps, u)
                steady(pool)
                k = list(FS)
                at = k.index(uname)
                outs = [FS[k[at + f]] for f in range(M)]
                pool.tensor_tensor(W["uy"], W[uname], W[yname], ALU.mult)
                pool.tensor_tensor(W["ur"], W[uname], W[rname], ALU.mult).then_inc(pool_step, 1)
                for out_, src in zip(outs[0:3], (uname, yname, sname)):
                    pool.tensor_tensor(out_, W[src][:, 0:UNIT], W[src][:, UNIT:BLK], ALU.add)
                pool.wait_ge(pool_step, POOL_STEPS * u + n0 + 1)
                steady(pool)
                pool.tensor_tensor(outs[3], W["uy"][:, 0:UNIT], W["uy"][:, UNIT:BLK], ALU.add)
                pool.tensor_tensor(outs[4], W["ur"][:, 0:UNIT], W["ur"][:, UNIT:BLK], ALU.add).then_inc(done, 1)
                pool.wait_ge(done, u + 1)
                pool.sem_inc(pool_step, 1)

            def k_features(u):
                features(u, 0, ("uk", "yk", "sk", "rk"), kfeat_ready, ksum_ps, kfeat_ready, (uk_ready, rk_ready))

            def q_features(u):
                features(u, 2, ("uq", "yq3", "sq", "rq"), qfeat_ready, qsum_ps, qfeat_ready, (uq_ready, rq_ready))

            def low(b, k, fill, lo, hi, done):
                pool.wait_ge(pT_used, 4 * b + fill + 1)
                steady(pool)
                pool.tensor_tensor(lo[:, k, :], xT_raw[:, k, :], hi[:, k, :].bitcast(F32), ALU.subtract).then_inc(done, 1)

            def low_xn(b):
                for k in range(NC):
                    low(b, k, k, xnT_lo, xnT_hi, xnT_lo_ready)

            def low_xf(b):
                for k in range(NC):
                    low(b, k, NC + k, xfT_lo, xfT_hi, xfT_lo_ready)

            def copy_stats(b, first=False):
                if not first:
                    pool.wait_ge(base_ready, b)
                pool.tensor_copy(stats_now[:, :], stats[:, bass.ds(b * (TPB * NS), 2 * TPB * NS)]).then_inc(now_copied, 1)

            def store_entries(b):
                pool.wait_ge(score_ready, 1)
                pool.wait_ge(place_ready, 1)
                pool.wait_ge(entries_stored, 16 * TPB * b)
                steady(pool)
                pool.tensor_copy(place_now[:, :], place[:, bass.ds(b * TPB, TPB)])
                pool.tensor_copy(entry_now[:, :], entry[:, bass.ds(b * TPB * 2, TPB * 2)]).then_inc(entry_copied, 1)
                pool.wait_ge(entry_copied, b + 1)
                steady(pool)
                for j in range(TPB):
                    pool.indirect_dma_start(
                        out=table, out_offset=bass.IndirectOffsetOnAxis(ap=place_now[:, j:j + 1], axis=0),
                        in_=entry_now[:, 2 * j:2 * j + 2], in_offset=None).then_inc(entries_stored, 16)

            def body(b, first, last):
                if not first:
                    copy_stats(b)
                k_features(2 * b)
                if first:
                    low(0, 1, NC + 1, xfT_lo, xfT_hi, xfT_lo_ready)
                q_features(2 * b)
                if not last:
                    low_xn(b + 1)
                    k_features(2 * b + 1)
                    q_features(2 * b + 1)
                    store_entries(b)
                    low_xf(b + 1)

            def expert_0_lo(n):
                pool.wait_ge(w_high, n + 1)
                steady(pool)
                split_lo(pool, 0, n)

            pool.wait_ge(stats_ready, 1)
            copy_stats(0, True)
            low_xn(0)
            for n, raw in enumerate((raw_gate, raw_up)):
                pool.wait_ge(gu_hi_ready, n + 1)
                at = slice(n * NC * I, (n + 1) * NC * I)
                pool.tensor_tensor(gu_lo[:, at], raw, gu_hi[:, at].bitcast(F32), ALU.subtract).then_inc(gu_lo_ready, 1)

            low(0, 0, NC, xfT_lo, xfT_hi, xfT_lo_ready)
            pool.wait_ge(stats_ready, GROUPS)
            for r in range(GB):
                pool.wait_ge(normed_stored[r], 16 * GROUPS)
            pool.wait_ge(pads_stored, 80)
            body(0, True, False)
            with pool.Fori(1, NB - 1) as b:
                body(b, False, False)
            body(NB - 1, False, True)

            store_entries(NB - 1)
            expert_0_lo(0)
            k_features(2 * NB - 1)
            q_features(2 * NB - 1)
            pool.wait_ge(entries_stored, 16 * NT)
            pool.dma_start(entries, table.rearrange("(t p) c -> p t c", p=P)).then_inc(entries_back, 16)
            expert_0_lo(1)
            pool.wait_ge(u_ps, NI * NB)
            expert_0_lo(2)

            for r in range(GB):
                pool.wait_ge(normed_stored[r], 16 * GROUPS)
            pool.wait_ge(pT_ps, 4 * NB)
            pool.wait_ge(entries_back, 16)

            def seat(into, set_, t, h):
                pool.tensor_copy(into[:, h:h + 1], sorted_entry[:, bass.ds(2 * t, 1)]).then_inc(set_, 1)

            def gather_row(t, i, h):
                seat(seat_x, seat_x_set, t, h)
                pool.wait_ge(seat_x_set, t + 1)
                steady(pool)
                pool.indirect_dma_start(out=e_rows[h], out_offset=None, in_=expert_rows,
                                        in_offset=bass.IndirectOffsetOnAxis(ap=seat_x[:, h:h + 1], axis=0)).then_inc(row_in[h], 16)

            def gather_rest(t, i, h):
                seat(seat_r, seat_r_set, t, h)
                pool.wait_ge(seat_r_set, t + 1)
                steady(pool)
                pool.indirect_dma_start(out=e_rest[h], out_offset=None, in_=rest_rows,
                                        in_offset=bass.IndirectOffsetOnAxis(ap=seat_r[:, h:h + 1], axis=0)).then_inc(rest_in[h], 16)

            def tile(t, i, h, rows_ahead=True, rest_ahead=True):
                if rows_ahead:
                    pool.wait_ge(xT_ps, t + 2)
                    pool.wait_ge(row_in[1 - h], 16 * (i + h) + 16)
                    steady(pool)
                    gather_row(t + 3, i + 1 + h, 1 - h)
                pool.wait_ge(out_stored[h], 16 * i)
                steady(pool)
                seat(seat_o, seat_o_set, t, h)
                pool.wait_ge(seat_o_set, t + 1)
                pool.wait_ge(y_ready, t + 1)
                steady(pool)
                pool.indirect_dma_start(out=out_rows, out_offset=bass.IndirectOffsetOnAxis(ap=seat_o[:, h:h + 1], axis=0),
                                        in_=e_y[h], in_offset=None, bounds_check=N - 1, oob_is_err=False).then_inc(out_stored[h], 16)
                if rest_ahead:
                    pool.wait_ge(rest_in[h], 16 * i + 16)
                    steady(pool)
                    gather_rest(t + 2, i + 1, h)

            gather_row(0, 0, 0)
            gather_row(1, 0, 1)
            pool.wait_ge(xT_ps, 1)
            pool.wait_ge(row_in[0], 16)
            gather_row(2, 1, 0)
            pool.wait_ge(quot_ready, 2 * NB)
            pool.wait_ge(rest_stored, 16 * NB)
            gather_rest(0, 0, 0)
            gather_rest(1, 0, 1)
            with pool.Fori(0, PAIRS) as i:
                tile(2 * i, i, 0)
                tile(2 * i + 1, i, 1)
            tile(ST - 3, PAIRS, 0, False, True)
            tile(ST - 2, PAIRS, 1, False, False)
            tile(ST - 1, PAIRS + 1, 0, False, False)
            pool.wait_ge(out_stored[0], 16 * (PAIRS + 2))
            pool.wait_ge(out_stored[1], 16 * (PAIRS + 1))

        @block.scalar
        def _(act):
            def roots(g):
                at = slice(g * GB * TPB, (g + 1) * GB * TPB)
                act.wait_ge(var_ready, g + 1)
                act.activation(small[:, 2:4, at], small[:, 0:2, at], ACT.Sqrt).then_inc(root_ready, 1)

            def affine(out_, ps, c):
                return act.activation(out_, ps, ACT.Identity, scale=ln_scale[:, c:c + 1], bias=ln_shift[:, c:c + 1])

            def keep_zT(b):
                act.wait_ge(turned, b + 1)
                if b >= 2:
                    act.wait_ge(logT_ps, b - 1)
                for c, ps in enumerate(((pK, pV), (pQ, pG))[b % 2]):
                    ins = affine(flat(ring_T[b % 2][:, :, :])[:, c * BLK:(c + 1) * BLK], ps[:, :], c)
                ins.then_inc(zT_ready, 1)

            def keep_logT(b):
                act.wait_ge(logT_ps, b + 1)
                act.wait_ge(logit_ps, b)
                act.activation(logT, pS[0:E, :], ACT.Copy).then_inc(logT_ready, 1)

            def keep_logits(b):
                act.wait_ge(logit_ps, b + 1)
                act.activation(logit[:, :, b * TPB:(b + 1) * TPB],
                               pR[:, 0:TPB * E].rearrange("p (j e) -> p e j", e=E), ACT.Copy).then_inc(logit_ready, 1)

            def normed(b, out_, k, done):
                for j in range(TPB):
                    at = (TPB + j) * NS + k
                    ins = act.activation(out_[:, j, :], x_next[:, j, :], ACT.Identity,
                                         scale=stats_now[:, at:at + 1], bias=stats_now[:, at + 1:at + 2])
                ins.then_inc(done, 1)

            def norm_next(b):
                act.wait_ge(x_next_in, 16 * b)
                act.wait_ge(now_copied, b)
                act.wait_ge(pT_ps, 4 * b)
                steady(act)
                normed(b, xn, 0, xn_ready)
                normed(b, z, 2, z_ready)

            def set_base(b, first):
                act.wait_ge(x_now_in, 16 * b + 16)
                act.wait_ge(now_copied, b + 1)
                if not first:
                    act.wait_ge(rest_done, 2 * b)
                    steady(act)
                for j in range(TPB):
                    at = j * NS
                    ins = act.activation(base[:, j, :], x_now[:, j, :], ACT.Identity,
                                         scale=stats_now[:, at + 4:at + 5], bias=stats_now[:, at + 1:at + 2])
                ins.then_inc(base_ready, 1)

            def keep_xn(b, k):
                act.wait_ge(pT_ps, 4 * b + k + 1)
                if not isinstance(b, int) or b:
                    act.wait_ge(xfT_lo_ready, 2 * b + (k - 1))
                    act.wait_ge(v_ps, 2 * b)
                    steady(act)
                act.activation(xT_raw[:, k, :], pT[:, :], ACT.Copy)
                act.activation(xnT_hi[:, k, :], pT[:, :], ACT.Copy).then_inc(pT_used, 1)

            def keep_xf(b, k):
                act.wait_ge(pT_ps, 4 * b + NC + k + 1)
                act.wait_ge(xnT_lo_ready, 2 * b + k + 1)
                act.wait_ge(u_ps, NI * b)
                steady(act)
                affine(xT_raw[:, k, :], pT[:, :], k)
                affine(xfT_hi[:, k, :], pT[:, :], k).then_inc(pT_used, 1)

            def keep_kq(u):
                for ps, have, used, name, done in ((pK, k_ps, uk_ready, "kraw", kraw_ready), (pQ, q_ps, uq_ready, "qraw", qraw_ready)):
                    act.wait_ge(have, u + 1)
                    act.wait_ge(used, u)
                    steady(act)
                    act.activation(W[name], ps[:, :], ACT.Copy).then_inc(done, 1)

            def k_squares(u):
                act.wait_ge(uk_ready, u + 1)
                steady(act)
                act.activation(W["yk"], W["uk"], ACT.Square, scale=0.25).then_inc(yk_ready, 1)
                act.wait_ge(yk_ready, u + 1)
                steady(act)
                act.activation(W["sk"], W["yk"], ACT.Square, bias=const("mhalf")).then_inc(sk_ready, 1)
                act.activation(W["rk"], W["yk"], ACT.Square, bias=const("mfive8")).then_inc(rk_ready, 1)

            def q_squares(u):
                act.wait_ge(uq_ready, u + 1)
                steady(act)
                act.activation(W["yq3"], W["uq"], ACT.Square, scale=0.25 * A3 ** 0.5).then_inc(yq3_ready, 1)
                act.activation(W["yq2"], W["uq"], ACT.Square, scale=0.25 * A2 ** 0.5).then_inc(yq2_ready, 1)
                act.wait_ge(yq3_ready, u + 1)
                steady(act)
                act.activation(W["rq"], W["yq3"], ACT.Square, bias=const("r5bias"), scale=A5 ** 0.5 / A3)
                act.activation(W["sq"], W["yq3"], ACT.Square, bias=const("s4bias"), scale=A4 ** 0.5 / A3).then_inc(rq_ready, 1)

            def widen(u):
                act.wait_ge(recip_ready, u + 1)
                act.wait_ge(spread_ps, u)
                steady(act)
                act.activation(recip_wide[:, :, :], recip[:, :].unsqueeze(2).to_broadcast([P, TPU * HEADS, HG]),
                               ACT.Copy).then_inc(wide_ready, 1)

            def round_num(b, a):
                act.wait_ge(quot_ready, 2 * b + (a + 1))
                act.wait_ge(out_ps, 2 * b)
                steady(act)
                act.activation(num_hi[:, a], num[:, a], ACT.Copy).then_inc(num_hi_ready, 1)

            def gate(b, n):
                act.wait_ge(g_ps, NI * b + n + 1)
                act.wait_ge(hid_ready, NI * b + n)
                steady(act)
                act.activation(silu[:, :], pG[:, :], ACT.Silu).then_inc(silu_ready, 1)

            def body(b, first, last):
                k_squares(2 * b)
                if not first:
                    widen(2 * b - 1)
                q_squares(2 * b)
                if first:
                    keep_xf(0, 1)
                if not last:
                    norm_next(b + 1)
                if not first:
                    round_num(b - 1, 1)
                keep_kq(2 * b + 1)
                set_base(b, first)
                if not last:
                    keep_xn(b + 1, 0)
                if first:
                    act.wait_ge(best_ready, 1)
                    act.wait_ge(zero_set, 3)
                    act.activation(entry[:, :].bitcast(F32).rearrange("p (t c) -> p t c", c=2)[:, :, 1:2], best.unsqueeze(2),
                                   ACT.Sigmoid).then_inc(score_ready, 1)
                gate(b, 0)
                if last:
                    act.wait_ge(v_ps, 2 * NB)
                    act.wait_ge(w_loaded, 1)
                    for n in range(PIECES):
                        split_hi(act, 0, n)
                if not last:
                    keep_xn(b + 1, 1)
                k_squares(2 * b + 1)
                gate(b, 1)
                q_squares(2 * b + 1)
                widen(2 * b)
                if not last:
                    keep_kq(2 * b + 2)
                gate(b, 2)
                gate(b, 3)
                round_num(b, 0)
                if not last:
                    keep_xf(b + 1, 0)
                    keep_xf(b + 1, 1)

            def first_block(out_, k, tiles):
                for j in tiles:
                    at = j * NS + k
                    ins = act.activation(out_[:, j, :], x_all[:, j, :], ACT.Identity,
                                         scale=stats[:, at:at + 1], bias=stats[:, at + 1:at + 2])
                return ins

            def round_in(s):
                act.wait_ge(turned_w, s + 1)
                act.activation(win_hi[:, :, s, :], pair((pU, pU, pT)[s][:, :]), ACT.Copy).then_inc(whi_ready, 1)

            def round_gu(n):
                act.wait_ge(raw_loaded, RAWS)
                act.activation(gu_hi[:, n * NC * I:(n + 1) * NC * I], (raw_gate, raw_up)[n], ACT.Copy).then_inc(gu_hi_ready, 1)

            roots(0)
            act.wait_ge(first_loaded, FIRSTS)
            for b in range(NB):
                keep_zT(b)
                if b == GB - 1:
                    roots(1)
                if b not in (0, GB):
                    keep_logT(b - 1)
                if b > 1:
                    keep_logits(b - 2)
                if b == GB - 1:
                    round_in(0)
                    act.wait_ge(stats_ready, 1)
                    first_block(xn, 0, range(TPB)).then_inc(xn_ready, 1)
                    keep_logT(b)
                elif b in (4, 5):
                    keep_xn(0, b - 4)
                elif b in (6, 7):
                    round_in(b - 5)
                    ins = first_block(z, 2, range(TPU * (b - 6), TPU * (b - 5)))
            ins.then_inc(z_ready, 1)
            round_gu(0)
            keep_logT(NB - 1)
            keep_logits(NB - 2)
            act.wait_ge(turned_w, 4)
            act.activation(wout_hi, pair(pU[:, :]), ACT.Copy).then_inc(wout_hi_ready, 1)
            keep_logits(NB - 1)
            round_gu(1)
            keep_xf(0, 0)
            act.wait_ge(const_set, 4)
            keep_kq(0)
            body(0, True, False)
            with act.Fori(1, NB - 1) as b:
                body(b, False, False)
            body(NB - 1, False, True)
            widen(2 * NB - 1)

            act.wait_ge(u_ps, NI * NB)
            act.wait_ge(w_loaded, 2)
            for n in range(PIECES):
                if n == 1:
                    round_num(NB - 1, 1)
                split_hi(act, 1, n)
            act.wait_ge(entries_back, 16)
            score = sorted_entry[:, :].bitcast(F32)

            def keep_xT(t, i, h):
                act.wait_ge(xT_ps, t + 1)
                act.wait_ge(xT_lo_ready, t)
                steady(act)
                for c in range(NC):
                    ins = affine(e_xT[:, c * P:(c + 1) * P], pT[:, c * P:(c + 1) * P], c)
                ins.then_inc(xT_kept, 1)
                act.wait_ge(xT_kept, t + 1)
                act.wait_ge(eu_ps[h], i)
                if isinstance(t, int) and t == 0:
                    act.wait_ge(out_ps, 2 * NB)
                steady(act)
                act.activation(e_xT_hi[h], e_xT, ACT.Copy).then_inc(xT_hi_ready, 1)

            def expert_gate(t, h):
                act.wait_ge(eg_ps, t + 1)
                act.wait_ge(ehid_ready, t)
                act.activation(e_silu, e_gate[h][:, :], ACT.Silu, scale=score[:, bass.ds(2 * t + 1, 1)]).then_inc(esilu_ready, 1)

            def keep_hT(t):
                act.wait_ge(hT_ps, t + 1)
                act.wait_ge(y_ps, t)
                steady(act)
                act.activation(e_hT_hi, pQ[:, :], ACT.Copy).then_inc(hT_hi_ready, 1)

            def tile(t, i, h, ahead=True, split=True):
                if split:
                    e = act.value_load(tile_split[0:1, bass.ds(t, 1)], min_val=0, max_val=E - 1)
                expert_gate(t, h)
                if ahead:
                    keep_xT(t + 1, i + h, 1 - h)
                if split:
                    with act.If(e > 0):
                        act.wait_ge(w_loaded, e + 1)
                        act.wait_ge(eu_ps[1 - h], i + h)
                        steady(act)
                        for n in range(PIECES - 1):
                            split_hi(act, e % SLOTS, n)
                keep_hT(t)
                if split:
                    with act.If(e > 0):
                        act.wait_ge(y_ps, t)
                        steady(act)
                        split_hi(act, e % SLOTS, PIECES - 1)

            keep_xT(0, 0, 0)
            act.wait_ge(quot_ready, 2 * NB)
            tile(0, 0, 0, split=False)
            with act.Fori(0, PAIRS) as i:
                tile(2 * i + 1, i, 1)
                tile(2 * i + 2, i + 1, 0)
            tile(ST - 2, PAIRS, 1)
            tile(ST - 1, PAIRS + 1, 0, False, False)

        @block.vector
        def _(dve):
            steps = [0]

            def stat_op(ins):
                steps[0] += 1
                ins.then_inc(stat_step, 1)
                dve.wait_ge(stat_step, steps[0])

            for g in range(GROUPS):
                at = slice(g * GB * TPB, (g + 1) * GB * TPB)
                tiles = range(at.start, at.stop)
                for t in tiles:
                    if t % TPB == 0:
                        dve.wait_ge(x_loaded[t // TPB], 16)
                    ins = dve.bn_stats(moments6[:, t, :], x_all[:, t, :])
                stat_op(ins)
                for t in tiles:
                    ins = dve.bn_aggr(moments[:, t, :], moments6[:, t, :])
                stat_op(ins)
                mean, var = moments[:, at, 0], moments[:, at, 1]
                v, root, guess, t0, t1 = (small[:, 2 * k:2 * k + 2, at] for k in range(5))
                both_rstd = stat[:, at, 0:3:2].rearrange("p t k -> p k t")
                stat_op(dve.tensor_scalar(v[:, 0, :], var, LN_EPS, None, ALU.add))
                dve.scalar_tensor_tensor(v[:, 1, :], v[:, 0, :], LN_EPS, v[:, 0, :], ALU.mult, ALU.add).then_inc(var_ready, 1)
                dve.wait_ge(var_ready, g + 1)
                dve.wait_ge(root_ready, g + 1)
                stat_op(dve.reciprocal(guess, root))
                stat_op(dve.tensor_tensor(t0, guess, guess, ALU.mult))
                stat_op(dve.tensor_tensor(t1, t0, v, ALU.mult))
                stat_op(dve.tensor_scalar(t0, t1, -0.5, 1.5, ALU.mult, ALU.add))
                stat_op(dve.tensor_tensor(both_rstd, guess, t0, ALU.mult))
                for b in range(g * GB, (g + 1) * GB):
                    r = b % GB
                    if g:
                        dve.wait_ge(normed_stored[r], 16 * g)
                        dve.wait_ge(turned, b - GB + 1)
                    for j in range(TPB):
                        t = TPB * b + j
                        ins = dve.tensor_scalar(ring[r][:, j, :], x_all[:, t, :], moments[:, t, 0:1], stat[:, t, 2:3],
                                                ALU.subtract, ALU.mult)
                    ins.then_inc(normed_ready, 1)
                for k, s in ((1, 0), (3, 2)):
                    dve.scalar_tensor_tensor(stat[:, at, k], mean, -1.0, stat[:, at, s], ALU.mult, ALU.mult)
                dve.tensor_scalar(stat[:, at, 4], stat[:, at, 0], 1.0, None, ALU.add).then_inc(stats_ready, 1)

            dve.wait_ge(in_loaded, INS)
            for r in range(2):
                ins = dve.tensor_copy(raw_out_c[:, r, :].rearrange("p (c h g) -> p c h g", c=NC, g=HG),
                                      raw_out[:, r, :].rearrange("p (h c g) -> p c h g", c=NC, g=HG))
            ins.then_inc(out_sorted, 1)

            for s in range(3):
                dve.wait_ge(whi_ready, s + 1)
                dve.tensor_tensor(win_lo[:, :, s, :], pair((pU, pU, pT)[s][:, :]), win_hi[:, :, s, :].bitcast(F32),
                                  ALU.subtract).then_inc(wlo_ready, 1)

            rsteps = [0]

            def route_op(ins):
                rsteps[0] += 1
                ins.then_inc(route_step, 1)
                dve.wait_ge(route_step, rsteps[0])

            def by_tile(ap):
                return ap.rearrange("p e t -> p t e")

            equal, ranked, onehot, upto, where, sums = (grids[:, k, :].rearrange("p (e t) -> p e t", e=E) for k in range(6))
            first = hid[:, 1, 64:64 + NT]
            seats_f = hid[:, 1, 96:96 + NT]
            tiles_i = hid[:, 1, 128:128 + E].bitcast(I32)
            tiles_f, starts = (hid[:, 1, 136 + 8 * k:144 + 8 * k] for k in range(2))
            ends = expert_ends[:, :]
            past = grids[0:1, 0:2, :].rearrange("p a b -> p (a b)")[:, 0:E * ST].rearrange("p (e t) -> p e t", e=E)
            expert, begins, follower = (grids[0:1, 3, 64 * k:64 * k + ST] for k in range(3))
            around = grids[0:1, 4, 0:ST]
            dve.wait_ge(logit_ready, NB)
            dve.wait_ge(const_loaded, CONSTS)
            dve.wait_ge(const_set, 4)
            dve.tensor_reduce(best, by_tile(logit[:, :, :]), AX, ALU.max).then_inc(best_ready, 1)
            dve.wait_ge(best_ready, 1)
            route_op(dve.tensor_tensor(equal, logit[:, :, :], best[:, None, :].to_broadcast([P, E, NT]), ALU.is_equal))
            route_op(dve.tensor_tensor(ranked, equal, rank, ALU.mult))
            route_op(dve.tensor_reduce(first, by_tile(ranked), AX, ALU.max))
            dve.tensor_tensor(onehot, ranked, first[:, None, :].to_broadcast([P, E, NT]), ALU.is_equal).then_inc(onehot_ready, 1)
            dve.wait_ge(wout_hi_ready, 1)
            dve.tensor_tensor(wout_lo, pair(pU[:, :]), wout_hi.bitcast(F32), ALU.subtract).then_inc(wout_lo_ready, 1)
            dve.wait_ge(before_ps, 1)
            flat_upto, flat_sums = upto.rearrange("p e t -> p (e t)"), sums.rearrange("p e t -> p (e t)")
            route_op(dve.tensor_tensor_scan(flat_upto, flat(tilemask), pR[:, 0:E * NT], 0.0, ALU.mult, ALU.add))
            route_op(dve.tensor_tensor(flat_sums, flat_upto, pR[:, 0:E * NT], ALU.subtract))
            route_op(dve.tensor_tensor(where.rearrange("p e t -> p (e t)"), flat_sums, pS[:, 0:E * NT], ALU.add))
            def places():
                route_op(dve.tensor_scalar(tiles_i, upto[:, :, NT - 1], float(P - 1), None, ALU.add))
                route_op(dve.tensor_scalar(tiles_i, tiles_i, P.bit_length() - 1, None, ALU.arith_shift_right))
                route_op(dve.tensor_scalar(tiles_f, tiles_i, 1.0, None, ALU.max))
                route_op(dve.tensor_tensor_scan(ends, tiles_f, tiles_f, 0.0, ALU.add, ALU.bypass))
                route_op(dve.tensor_tensor(starts, ends, tiles_f, ALU.subtract))
                route_op(dve.tensor_scalar(starts, starts, float(P), None, ALU.mult))
                route_op(dve.tensor_tensor(sums, where, starts.unsqueeze(2).to_broadcast([P, E, NT]), ALU.add))
                route_op(dve.tensor_tensor(where, sums, onehot, ALU.mult))
                route_op(dve.tensor_reduce(seats_f, by_tile(where), AX, ALU.add))
                dve.tensor_copy(place[:, :], seats_f).then_inc(place_ready, 1)

            def tile_map():
                route_op(dve.tensor_tensor(past, const("tileno", 1).rearrange("p (e t) -> p e t", e=E),
                                           ends[0:1, :].unsqueeze(2).to_broadcast([1, E, ST]), ALU.is_ge))
                route_op(dve.tensor_reduce(expert, by_tile(past), AX, ALU.add))
                route_op(dve.tensor_scalar(expert, expert, float(E - 1), None, ALU.min))
                route_op(dve.scalar_tensor_tensor(around[:, 1:ST], expert[:, 1:ST], float(E), expert[:, 0:ST - 1], ALU.mult, ALU.add))
                route_op(dve.tensor_scalar(around[:, 0:1], expert[:, 0:1], float(E), None, ALU.mult))
                route_op(dve.scalar_tensor_tensor(tile_expert[:, 0:ST - 1], expert[:, 1:ST], float(E * E), around[:, 0:ST - 1], ALU.mult, ALU.add))
                dve.tensor_copy(tile_expert[:, ST - 1:ST], around[:, ST - 1:ST])
                route_op(dve.memset(begins[:, 0:1], 0.0))
                route_op(dve.tensor_tensor(begins[:, 1:ST], expert[:, 1:ST], expert[:, 0:ST - 1], ALU.subtract))
                route_op(dve.tensor_scalar(follower, expert, 1.0, None, ALU.add))
                route_op(dve.tensor_tensor(follower, follower, begins, ALU.mult))
                route_op(dve.tensor_scalar(begins, follower, float(E), None, ALU.is_lt))
                dve.tensor_tensor(tile_split[:, :], follower, begins, ALU.mult).then_inc(map_ready, 1)

            DEN_STEPS = 5

            def sums_of_k(u, b, first):
                dve.wait_ge(ksum_ps, u + 1)
                dve.wait_ge(prefix_ps, u)
                dve.tensor_tensor(ksb[:, :], ksum_at, const("kbias"), ALU.add).then_inc(den_step, 1)
                dve.wait_ge(den_step, DEN_STEPS * u + 1)
                if not first:
                    dve.wait_ge(acc_kept, b)
                dve.tensor_tensor(acc[:, R:2 * R], acc[:, 0:R], ksb[:, 0:R], ALU.add).then_inc(ksb_ready, 1)

            def denominator(u, b, keep):
                dve.wait_ge(qsum_ps, u + 1)
                dve.tensor_tensor(qsb[:, :], qsum_at, const("qbias"), ALU.add).then_inc(qsb_ready, 1)
                dve.wait_ge(prefix_ps, u + 1)
                dve.tensor_tensor(acc[:, 0:R], acc[:, R:2 * R], ksb[:, R:2 * R], ALU.add).then_inc(den_step, 1)
                dve.wait_ge(qsb_ready, u + 1)
                dve.tensor_tensor(prod[:, :], qsb[:, :], prefix_at, ALU.mult).then_inc(den_step, 1)
                dve.wait_ge(den_step, DEN_STEPS * u + 3)
                if keep:
                    dve.tensor_scalar(acc[:, 0:R], acc[:, 0:R], KEEP(b), None, ALU.mult).then_inc(acc_kept, 1)
                dve.wait_ge(recip_ready, u)
                dve.tensor_reduce(den[:, :], prod[:, :].rearrange("p (j m h) -> p j h m", j=TPU, m=M), AX,
                                  ALU.add).then_inc(den_step, 1)
                dve.wait_ge(den_step, DEN_STEPS * u + 4)
                dve.tensor_scalar(den[:, :], den[:, :], DEN_EPS, None, ALU.add).then_inc(den_step, 1)
                dve.wait_ge(den_step, DEN_STEPS * u + 5)
                dve.wait_ge(wide_ready, u)
                dve.reciprocal(recip[:, :], den[:, :]).then_inc(recip_ready, 1)

            def quotient(u, a):
                dve.wait_ge(spread_ps, u + 1)
                dve.tensor_tensor(num[:, a], num[:, a], spread_at.unsqueeze(1).to_broadcast([P, NC, UNIT]),
                                  ALU.mult).then_inc(quot_ready, 1)

            def low_num(b, a):
                dve.wait_ge(num_hi_ready, 2 * b + (a + 1))
                dve.tensor_tensor(num_lo[:, a], num[:, a], num_hi[:, a].bitcast(F32), ALU.subtract).then_inc(num_lo_ready, 1)

            def KEEP(b):
                at = CONST["keep"][0] + 1
                return cst[:, bass.ds(b + at, 1)]

            def hidden(b, n):
                dve.wait_ge(silu_ready, NI * b + n + 1)
                dve.wait_ge(u_ps, NI * b + n + 1)
                dve.wait_ge(out_ps, 2 * b)
                dve.tensor_tensor(hid[:, n, :], silu[:, :], pU[:, :], ALU.mult).then_inc(hid_ready, 1)

            def add_rest(b):
                dve.wait_ge(base_ready, b + 1)
                dve.wait_ge(rest_stored, 16 * b)
                for k, ps in enumerate((pG, pU)):
                    dve.wait_ge(out_ps, 2 * b + k + 1)
                    dve.tensor_tensor(flat(rest[:, 2 * k:2 * k + 2, :]), flat(base[:, 2 * k:2 * k + 2, :]), ps[:, :],
                                      ALU.add).then_inc(rest_done, 1)

            count = [0]
            UNIT_STEPS = 19

            def unit(b, a, first):
                u = 2 * b + a
                count[0] = 0

                def step(ins):
                    ins.then_inc(dve_step, 1)
                    count[0] += 1
                    return count[0]

                def need(k):
                    dve.wait_ge(dve_step, UNIT_STEPS * u + k)

                def term(m):
                    return terms[:, m, :, 1:UNIT + 1]

                def sum_(m):
                    return run[:, m, :, 1:UNIT + 1]

                def running(m):
                    return step(dve.tensor_tensor_scan(flat(run[:, m]), const("restart"), flat(terms[:, m]), 0.0, ALU.mult, ALU.add))

                uk, yk, sk, rk, uq, yq3, yq2, sq, rq, t1, t2, t3 = (
                    pair(W[n]) for n in ("uk", "yk", "sk", "rk", "uq", "yq3", "yq2", "sq", "rq", "t1", "t2", "t3"))
                v = pair(pV[:, :])
                dve.wait_ge(kraw_ready, u + 1)
                dve.wait_ge(kfeat_ready, u)
                dve.tensor_scalar(W["uk"], W["kraw"], -CLIP, CLIP, ALU.max, ALU.min).then_inc(uk_ready, 1)
                dve.wait_ge(qraw_ready, u + 1)
                dve.wait_ge(qfeat_ready, u)
                dve.tensor_scalar(W["uq"], W["qraw"], -CLIP, CLIP, ALU.max, ALU.min).then_inc(uq_ready, 1)
                dve.wait_ge(v_ps, u + 1)
                dve.wait_ge(uk_ready, u + 1)
                need(0)
                g1 = step(dve.tensor_tensor(term(0), uk, v, ALU.mult))
                if a == 0 and first:
                    places()
                dve.wait_ge(yk_ready, u + 1)
                g2 = step(dve.scalar_tensor_tensor(term(1), yk, -0.5, v, ALU.add, ALU.mult))
                need(g1)
                r1 = running(0)
                g3 = step(dve.scalar_tensor_tensor(term(2), yk, -0.75, term(0), ALU.add, ALU.mult))
                need(g2)
                r2 = running(1)
                if a == 1:
                    denominator(u - 1, b, False)
                elif not first:
                    denominator(u - 1, b - 1, True)
                dve.wait_ge(rk_ready, u + 1)
                g4 = dve.scalar_tensor_tensor(term(3), sk, -0.125, v, ALU.add, ALU.mult).then_inc(v_used, 1)
                g5 = step(dve.scalar_tensor_tensor(term(4), rk, -5.0 / 64, term(0), ALU.add, ALU.mult))
                if a == 1:
                    hidden(b, 1)
                need(g3)
                r3 = running(2)
                dve.wait_ge(v_used, u + 1)
                r4 = running(3)
                need(g5)
                r5 = running(4)
                if a == 1 or not first:
                    quotient(u - 1, 1 - a)
                dve.wait_ge(yq3_ready, u + 1)
                need(r3)
                p3 = step(dve.scalar_tensor_tensor(t1, yq3, -0.75 * A3, sum_(2), ALU.add, ALU.mult))
                dve.wait_ge(rq_ready, u + 1)
                need(r5)
                p5 = step(dve.scalar_tensor_tensor(t2, rq, -5.0 / 64 * A5, sum_(4), ALU.add, ALU.mult))
                p2 = step(dve.scalar_tensor_tensor(t3, yq2, -0.5 * A2, sum_(1), ALU.add, ALU.mult))
                need(p5)
                a1 = step(dve.tensor_tensor(t1, t1, t2, ALU.add))
                if a == 0 and not first:
                    low_num(b - 1, 1)
                    add_rest(b - 1)
                if a == 1:
                    hidden(b, 2)
                need(a1)
                p4 = step(dve.scalar_tensor_tensor(t2, sq, -0.125 * A4, sum_(3), ALU.add, ALU.mult))
                a2 = step(dve.tensor_tensor(t1, t1, sum_(0), ALU.add))
                need(p4)
                a3 = step(dve.tensor_tensor(t3, t3, t2, ALU.add))
                need(a2)
                a4 = step(dve.tensor_tensor(t1, t1, uq, ALU.mult))
                if a == 0:
                    sums_of_k(u, b, first)
                else:
                    hidden(b, 3)
                need(a4)
                dve.wait_ge(out_ps, 2 * b)
                numer = step(dve.tensor_tensor(num[:, a], t1, t3, ALU.add))
                if a == 0:
                    step(dve.tensor_copy(terms[:, :, :, 0:1], run[:, :, :, UNIT:UNIT + 1]))
                else:
                    step(dve.tensor_scalar(terms[:, :, :, 0:1], run[:, :, :, UNIT:UNIT + 1], KEEP(b), None, ALU.mult))
                if a == 0 and first:
                    tile_map()
                if a == 0:
                    hidden(b, 0)
                else:
                    low_num(b, 0)
                    sums_of_k(u, b, True)
                assert count[0] == UNIT_STEPS, count[0]

            dve.wait_ge(zero_set, 3)
            dve.wait_ge(pads_stored, 80)
            for r in range(GB):
                dve.wait_ge(normed_stored[r], 16 * GROUPS)
            unit(0, 0, True)

            unit(0, 1, True)
            with dve.Fori(1, NB) as b:
                unit(b, 0, False)
                unit(b, 1, False)
            denominator(2 * NB - 1, NB - 1, True)
            quotient(2 * NB - 1, 1)
            low_num(NB - 1, 1)
            dve.wait_ge(w_low, PIECES)
            for n in range(PIECES - 1):
                dve.wait_ge(w_high, PIECES + n + 1)
                split_lo(dve, 1, n)
            add_rest(NB - 1)

            score = sorted_entry[:, :].bitcast(F32)
            dve.wait_ge(entries_back, 16)

            def expert_hidden(t, i, h):
                dve.wait_ge(esilu_ready, t + 1)
                dve.wait_ge(eu_ps[h], i + 1)
                if not isinstance(t, int) or t > 1:
                    dve.wait_ge(hT_ps, t - 1)
                dve.scalar_tensor_tensor(e_hid[h], e_up[h][:, :], score[:, bass.ds(2 * t + 1, 1)], e_silu,
                                         ALU.mult, ALU.mult).then_inc(ehid_ready, 1)

            def expert_out(t, i, h):
                dve.wait_ge(y_ps, t + 1)
                dve.wait_ge(rest_in[h], 16 * i + 16)
                dve.wait_ge(out_stored[h], 16 * i)
                dve.tensor_tensor(e_y[h], e_rest[h], pS[:, 0:D], ALU.add).then_inc(y_ready, 1)

            def low_xT(t, h):
                dve.wait_ge(xT_hi_ready, t + 1)
                dve.tensor_tensor(e_xT_lo[h], e_xT, e_xT_hi[h].bitcast(F32), ALU.subtract).then_inc(xT_lo_ready, 1)

            def low_hT(t):
                dve.wait_ge(hT_hi_ready, t + 1)
                dve.tensor_tensor(e_hT_lo, pQ[:, :], e_hT_hi.bitcast(F32), ALU.subtract).then_inc(hT_lo_ready, 1)

            def tile(t, i, h, ahead=True, behind=True, split=True):
                if split:
                    e = dve.value_load(tile_split[0:1, bass.ds(t, 1)], min_val=0, max_val=E - 1)
                expert_hidden(t, i, h)
                if ahead:
                    low_xT(t + 1, 1 - h)
                if behind:
                    expert_out(t - 1, i - 1 + h, 1 - h)
                if split:
                    with dve.If(e > 0):
                        dve.wait_ge(w_high, e * PIECES + 1)
                        split_lo(dve, e % SLOTS, 0)
                low_hT(t)
                if split:
                    with dve.If(e > 0):
                        for n in range(1, PIECES):
                            dve.wait_ge(w_high, e * PIECES + (n + 1))
                            split_lo(dve, e % SLOTS, n)

            low_xT(0, 0)
            dve.wait_ge(w_high, 2 * PIECES)
            split_lo(dve, 1, PIECES - 1)
            tile(0, 0, 0, behind=False, split=False)
            with dve.Fori(0, PAIRS) as i:
                tile(2 * i + 1, i, 1)
                tile(2 * i + 2, i + 1, 0)
            tile(ST - 2, PAIRS, 1)
            tile(ST - 1, PAIRS + 1, 0, ahead=False, split=False)
            expert_out(ST - 1, PAIRS + 1, 0)

        @block.tensor
        def _(pe):
            pe.wait_ge(first_loaded, FIRSTS)

            def turn(b, g, r):
                pe.wait_ge(normed_ready, b + 1)
                if not (isinstance(b, int) and b < 2):
                    pe.wait_ge(zT_ready, b - 1)
                for c, ps in enumerate(((pK, pV), (pQ, pG))[r % 2]):
                    for j in range(TPB):
                        ins = pe.transpose(ps[:, j * P:(j + 1) * P], ring[r][:, j, c * P:(c + 1) * P], ident)
                ins.then_inc(turned, 1)

            def route(b, r):
                zT = flat(ring_T[r % 2][:, :, :])
                pe.wait_ge(zT_ready, b + 1)
                pe.wait_ge(logT_ready, b)
                for c in range(NC):
                    ins = pe.matmul(pS[0:E, :], router[:, c, :], zT[:, c * BLK:(c + 1) * BLK], start=(c == 0), stop=(c == NC - 1))
                ins.then_inc(logT_ps, 1)

            def turn_logits(b):
                pe.wait_ge(logT_ready, b + 1)
                pe.wait_ge(logit_ready, b)
                steady(pe)
                for j in range(TPB):
                    ins = pe.transpose(pR[:, j * E:(j + 1) * E], logT[:, j * P:(j + 1) * P], ident[0:E, 0:E])
                ins.then_inc(logit_ps, 1)

            def product(ps, terms_):
                n = 3 * len(terms_)
                k = 0
                for lh, ll, rh, rl in terms_:
                    for a, b_ in ((ll, rh), (lh, rl), (lh, rh)):
                        ins = pe.matmul(ps, a, b_, start=(k == 0), stop=(k == n - 1))
                        k += 1
                return ins

            def turn_block(b, k, src, ready, fill):
                pe.wait_ge(ready, b + 1)
                pe.wait_ge(pT_used, 4 * b + fill)
                for j in range(TPB):
                    ins = pe.transpose(pT[:, j * P:(j + 1) * P], src[:, j, k * P:(k + 1) * P], ident)
                ins.then_inc(pT_ps, 1)

            def turn_xn(b, k):
                turn_block(b, k, xn, xn_ready, k)

            def turn_z(b, k):
                turn_block(b, k, z, z_ready, NC + k)

            def project(b, a, some=(0, 1, 2)):
                u = 2 * b + a
                tok = slice(a * UNIT, (a + 1) * UNIT)
                pe.wait_ge(xnT_lo_ready, 2 * b + 2)
                kqv = ((pK, 1, kraw_ready, k_ps), (pQ, 0, qraw_ready, q_ps), (pV, 2, v_used, v_ps))
                for ps, part, free, done in [kqv[n] for n in some]:
                    pe.wait_ge(free, u)
                    for c in range(NC):
                        cols = slice(c * P, (c + 1) * P)
                        ins = product(ps[:, c * UNIT:(c + 1) * UNIT],
                                      [(win_hi[:, k, part, cols], win_lo[:, k, part, cols], xnT_hi[:, k, tok], xnT_lo[:, k, tok])
                                       for k in range(NC)])
                    ins.then_inc(done, 1)

            def gate_up(b, n):
                if n == 0:
                    pe.wait_ge(xfT_lo_ready, 2 * b + 2)
                    pe.wait_ge(rest_done, 2 * b)
                for ps, part, free, done in ((pG, 0, silu_ready, g_ps), (pU, 1, hid_ready, u_ps)):
                    pe.wait_ge(free, NI * b + n)
                    terms_ = []
                    for k in range(NC):
                        at = part * NC * I + k * I + n * P
                        terms_.append((gu_hi[:, at:at + P], gu_lo[:, at:at + P], xfT_hi[:, k, :], xfT_lo[:, k, :]))
                    product(ps[:, :], terms_).then_inc(done, 1)

            def head_sums(u, side):
                names = list(FS)[side * M:(side + 1) * M]
                out_, ready, mat, done = ((ksum_at, kfeat_ready, "ksum", ksum_ps), (qsum_at, qfeat_ready, "qsum", qsum_ps))[side]
                pe.wait_ge(ready, u + 1)
                pe.wait_ge(qsb_ready, u)
                for j in range(TPU):
                    for f, name in enumerate(names):
                        at = CONST[mat][0] + f * R
                        ins = pe.matmul(out_[:, j * R:(j + 1) * R], FS[name][:, j * P:(j + 1) * P], cst[:, at:at + R],
                                        start=(f == 0), stop=(f == M - 1))
                ins.then_inc(done, 1)

            def prefix(u):
                pe.wait_ge(ksb_ready, u + 1)
                pe.wait_ge(quot_ready, u)
                pe.matmul(prefix_at, const("upto"), ksb[:, :], start=True, stop=False)
                pe.matmul(prefix_at, const("ones"), acc[:, :], start=False, stop=True).then_inc(prefix_ps, 1)

            def spread(u):
                pe.wait_ge(wide_ready, u + 1)
                for j in range(TPU):
                    ins = pe.transpose(spread_at[:, j * P:(j + 1) * P], flat(recip_wide[:, j * HEADS:(j + 1) * HEADS, :]), ident)
                ins.then_inc(spread_ps, 1)

            def down_shared(b, k):
                pe.wait_ge(hid_ready, NI * b + NI)
                for j in range(TPU):
                    at = (TPU * k + j) * P
                    for n in range(NI):
                        pe.matmul((pG, pU)[k][:, j * D:(j + 1) * D], hid[:, n, at:at + P], down_s[:, n, :],
                                  start=(j == 0 and n == 0), stop=False, skip_group_check=True)

            def project_out(b):
                for k, ps in enumerate((pG, pU)):
                    pe.wait_ge(num_lo_ready, 2 * b + (k + 1))
                    for j in range(TPU):
                        tok = slice(j * P, (j + 1) * P)
                        for c in range(NC):
                            for lhs, rhs in ((num_lo, wout_hi), (num_hi, wout_lo), (num_hi, wout_hi)):
                                ins = pe.matmul(ps[:, j * D:(j + 1) * D], lhs[:, k, c, tok], rhs[:, c, :], start=False,
                                                stop=(c == NC - 1 and rhs is wout_hi and lhs is num_hi), skip_group_check=True)
                    ins.then_inc(out_ps, 1)

            def body(b, first, last):
                if not first:
                    spread(2 * b - 1)
                    down_shared(b - 1, 1)
                project(b, 1)
                if not first:
                    project_out(b - 1)
                head_sums(2 * b, 0)
                if not last:
                    turn_xn(b + 1, 0)
                gate_up(b, 0)
                if not last:
                    turn_xn(b + 1, 1)
                prefix(2 * b)
                head_sums(2 * b, 1)
                gate_up(b, 1)
                if not last:
                    project(b + 1, 0)
                spread(2 * b)
                gate_up(b, 2)
                gate_up(b, 3)
                if not last:
                    turn_z(b + 1, 0)
                head_sums(2 * b + 1, 0)
                if not last:
                    turn_z(b + 1, 1)
                prefix(2 * b + 1)
                head_sums(2 * b + 1, 1)
                down_shared(b, 0)

            def turn_in(s):
                for k in range(NC):
                    for c in range(NC):
                        ins = pe.transpose((pU, pU, pT)[s][:, k * D + c * P:k * D + (c + 1) * P], raw_in[:, s, c, k * P:(k + 1) * P], ident)
                ins.then_inc(turned_w, 1)

            turn(0, 0, 0)
            turn(1, 0, 1)
            route(0, 0)
            turn(2, 0, 2)
            turn_logits(0)
            route(1, 1)
            turn(3, 0, 3)
            pe.wait_ge(in_loaded, INS)
            turn_logits(1)
            route(2, 2)
            turn_in(0)
            turn_logits(2)
            route(3, 3)
            for b in range(GB, NB):
                turn(b, b // GB, b % GB)
                if b < GB + NC:
                    turn_xn(0, b - GB)
                if b > GB:
                    turn_logits(b - 2)
                    route(b - 1, (b - 1) % GB)
                if b == NB - 2:
                    pe.wait_ge(wlo_ready, 1)
                    turn_in(1)
            pe.wait_ge(pT_used, 2)
            turn_in(2)
            turn_logits(NB - 2)
            route(NB - 1, GB - 1)
            pe.wait_ge(out_sorted, 1)
            pe.wait_ge(wlo_ready, 2)
            for c in range(NC):
                for r in range(2):
                    ins = pe.transpose(pU[:, c * D + r * P:c * D + (r + 1) * P], raw_out_c[:, r, c * P:(c + 1) * P], ident)
            ins.then_inc(turned_w, 1)
            pe.wait_ge(wlo_ready, 3)
            turn_z(0, 0)
            turn_logits(NB - 1)
            pe.wait_ge(zT_ready, NB)
            project(0, 0, (0,))

            pe.wait_ge(onehot_ready, 1)
            pe.wait_ge(const_loaded, CONSTS)
            pe.wait_ge(const_set, 4)
            pe.matmul(pS[:, 0:E * NT], const("before"), grids[:, 2, :], start=True, stop=True)
            pe.matmul(pR[:, 0:E * NT], const("ones"), grids[:, 2, :], start=True, stop=True).then_inc(before_ps, 1)

            project(0, 0, (1, 2))
            turn_z(0, 1)
            pe.wait_ge(wout_lo_ready, 1)
            pe.wait_ge(gu_lo_ready, 2)
            pe.wait_ge(down_loaded, 16)
            body(0, True, False)
            with pe.Fori(1, NB - 1) as b:
                body(b, False, False)
            body(NB - 1, False, True)
            spread(2 * NB - 1)
            down_shared(NB - 1, 1)


            def turn_rows(t, i, h):
                pe.wait_ge(row_in[h], 16 * i + 16)
                pe.wait_ge(xT_kept, t)
                for c in range(NC):
                    ins = pe.transpose(pT[:, c * P:(c + 1) * P], e_rows[h][:, c * P:(c + 1) * P], ident)
                ins.then_inc(xT_ps, 1)

            def split_product(ps, lhs_hi, lhs_lo, at, width, parts):
                passes = [(lhs, part, k) for lhs, part in ((lhs_hi, 0), (lhs_hi, 1), (lhs_lo, 0)) for k in range(parts)]
                for n, (lhs, part, k) in enumerate(passes):
                    ins = pe.matmul(ps, lhs[:, k * P:(k + 1) * P], rounded[:, bass.ds(at + (part * WCOLS + k * width), width)],
                                    start=(n == 0), stop=(n == len(passes) - 1))
                return ins

            def up_or_gate(t, h, part, at):
                ps, done = ((e_gate[h], eg_ps), (e_up[h], eu_ps[h]))[part]
                split_product(ps[:, :], e_xT_hi[h], e_xT_lo[h], at + part * PIECE, I, NC).then_inc(done, 1)

            def turn_hidden(t, h):
                pe.wait_ge(ehid_ready, t + 1)
                pe.wait_ge(hT_lo_ready, t)
                for n in range(NI):
                    ins = pe.transpose(pQ[:, n * P:(n + 1) * P], e_hid[h][:, n * P:(n + 1) * P], ident)
                ins.then_inc(hT_ps, 1)

            def down(t, at):
                pe.wait_ge(hT_lo_ready, t + 1)
                pe.wait_ge(y_ready, t)
                split_product(pS[:, 0:D], e_hT_hi, e_hT_lo, at + 2 * PIECE, D, NI).then_inc(y_ps, 1)

            def step(t, i, h, ahead=True, behind=True):
                experts_now = pe.value_load(tile_expert[0:1, bass.ds(t, 1)], min_val=0, max_val=E ** 3 - 1)

                def column(e):
                    return (e % SLOTS) * (2 * WCOLS)

                if ahead:
                    turn_rows(t + 1, i + h, 1 - h)
                up_or_gate(t, h, 1, column(experts_now // E))
                if behind:
                    down(t - 1, column(experts_now))
                turn_hidden(t, h)
                if ahead:
                    e = experts_now // E ** 2
                    pe.wait_ge(w_low, e * PIECES + PIECES)
                    steady(pe)
                    pe.wait_ge(xT_lo_ready, t + 2)
                    up_or_gate(t + 1, 1 - h, 0, column(e))

            turn_rows(0, 0, 0)
            project_out(NB - 1)
            pe.wait_ge(map_ready, 1)
            pe.wait_ge(w_low, PIECES)
            pe.wait_ge(xT_lo_ready, 1)
            up_or_gate(0, 0, 0, 0)
            pe.wait_ge(rest_done, 2 * NB)
            step(0, 0, 0, behind=False)
            with pe.Fori(0, PAIRS // 2) as q:
                for k in range(4):
                    step(4 * q + (k + 1), 2 * q + (k + 1) // 2, (k + 1) % 2)
            step(ST - 2, PAIRS, 1)
            step(ST - 1, PAIRS + 1, 0, ahead=False)
            down(ST - 1, pe.value_load(tile_expert[0:1, ST - 1:ST], min_val=0, max_val=E ** 2 - 1) // E % SLOTS * (2 * WCOLS))


_INS = ["L0_attn_x", "L0_attn_W_in", "L0_attn_W_out", "L0_ffn_ln_w", "L0_ffn_ln_b", "L0_ffn_router_w", "L0_ffn_gate_w",
        "L0_ffn_up_w", "L0_ffn_down_w", "L0_ffn_sh_gate", "L0_ffn_sh_up", "L0_ffn_sh_down"]


def kernel(**inputs):
    import numpy as _np
    import concourse.bacc as _bacc
    from concourse import mybir as _mybir
    from concourse.bass_utils import run_bass_kernel_spmd as _run

    nc = _bacc.Bacc("TRN2", target_bir_lowering=False, num_devices=1)
    arrays, args = {"constants": constants()}, []
    for name in _INS:
        arrays[name] = _np.ascontiguousarray(inputs[name])
    for name, a in arrays.items():
        args.append(nc.dram_tensor(name, a.shape, _mybir.dt.from_np(a.dtype), kind="ExternalInput").ap())
    out = nc.dram_tensor("out", (B, S, D), _mybir.dt.float32, kind="ExternalOutput").ap()
    token_layer_kernel(nc, *args, out)
    r = _run(nc, [arrays], core_ids=[0])
    return r.results[0]["out"]
```
